# Optimizing a Trainium2 kernel written in Bass

```python
import numpy as np
import jax
import jax.numpy as jnp

def _softmax(x, axis=-1):
    return jax.nn.softmax(x, axis=axis)

def _gelu(x):
    return jax.nn.gelu(x, approximate=True)

def _silu(x):
    return jax.nn.silu(x)

def _sigmoid(x):
    return jax.nn.sigmoid(x)

def _layernorm(x, axis=-1, eps=1e-05):
    m = jnp.mean(x, axis=axis, keepdims=True)
    v = jnp.var(x, axis=axis, keepdims=True)
    return (x - m) / jnp.sqrt(v + eps)

def _scatter_add(tgt, idx, src, axis=0):
    return tgt.at[idx].add(src)

def _segment_sum(src, seg, n):
    return jax.ops.segment_sum(src, seg, n)
kernel_name = 'mk_prb_d1_jaxref_r4_082f7a'

def setup_inputs(seed: int=0):
    np.random.seed(seed)
    _w = jnp.asarray

    def _L0_attn_setup():
        import jax, jax.numpy as jnp
        import numpy as np
        B, SQ, HIDDEN = (2, 512, 512)
        HEADS, GROUPS, KVC = (16, 4, 128)
        HPG = HEADS // GROUPS
        LAYER_INDEX = 1
        SCALE = KVC ** (-0.5)
        key = jax.random.key(seed)
        k1, k2, k3, k4 = jax.random.split(key, 4)
        return {'x': jax.random.normal(k1, (B, SQ, HIDDEN), jnp.float32), 'w_q': jax.random.normal(k2, (HIDDEN, HEADS * KVC), jnp.float32) * 0.02, 'w_kv': jax.random.normal(k3, (HIDDEN, 2 * GROUPS * KVC), jnp.float32) * 0.02, 'w_dense': jax.random.normal(k4, (HEADS * KVC, HIDDEN), jnp.float32) * 0.02}
    _L0_attn_in = _L0_attn_setup()

    def _L0_ffn_setup():
        import jax, jax.numpy as jnp
        import numpy as np
        D = 512
        M = 256
        E = 32
        K = 6
        G = 8
        KG = 4
        SH = 512
        SCALE = 2.5

        def _route(xf, Wr, br):
            T = xf.shape[0]
            s = jax.nn.sigmoid(xf @ Wr.T + br)
            sg = s.reshape(T, G, E // G)
            group_w = jax.lax.top_k(sg, 2)[0].sum(-1)
            top_g = jax.lax.top_k(group_w, KG)[1]
            gmask = jnp.zeros((T, G), bool).at[jnp.arange(T)[:, None], top_g].set(True)
            masked = jnp.where(gmask[:, :, None], sg, 0.0).reshape(T, E)
            idx = jax.lax.top_k(masked, K)[1]
            w = jnp.take_along_axis(s, idx, axis=1)
            w = w / (w.sum(-1, keepdims=True) + 1e-20)
            return (idx, w * SCALE)
        key = jax.random.key(seed)
        ks = jax.random.split(key, 7)
        w = 0.02
        return {'hidden_tensor': jax.random.normal(ks[0], (2, 512, D), dtype=jnp.float32), 'Wr': jax.random.normal(ks[1], (E, D), dtype=jnp.float32) * w, 'br': jax.random.normal(ks[2], (E,), dtype=jnp.float32) * w, 'W1': jax.random.normal(ks[3], (E, M, D), dtype=jnp.float32) * w, 'W2': jax.random.normal(ks[4], (E, D, M), dtype=jnp.float32) * w, 'Ws1': jax.random.normal(ks[5], (SH, D), dtype=jnp.float32) * w, 'Ws2': jax.random.normal(ks[6], (D, SH), dtype=jnp.float32) * w}
    _L0_ffn_in = _L0_ffn_setup()
    _d = {'L0_attn_x': _L0_attn_in['x'], 'L0_attn_w_q': _L0_attn_in['w_q'], 'L0_attn_w_kv': _L0_attn_in['w_kv'], 'L0_attn_w_dense': _L0_attn_in['w_dense'], 'L0_ffn_Wr': _L0_ffn_in['Wr'], 'L0_ffn_br': _L0_ffn_in['br'], 'L0_ffn_W1': _L0_ffn_in['W1'], 'L0_ffn_W2': _L0_ffn_in['W2'], 'L0_ffn_Ws1': _L0_ffn_in['Ws1'], 'L0_ffn_Ws2': _L0_ffn_in['Ws2']}
    _x0 = _d['L0_attn_x']
    _d['L0_attn_x'] = jax.random.normal(jax.random.fold_in(jax.random.key(seed), 1), (2, 1024, 512), dtype=_x0.dtype)
    del _x0
    return _d

def reference(L0_attn_x, L0_attn_w_q, L0_attn_w_kv, L0_attn_w_dense, L0_ffn_Wr, L0_ffn_br, L0_ffn_W1, L0_ffn_W2, L0_ffn_Ws1, L0_ffn_Ws2):

    def _L0_attn_ref(x, w_q, w_kv, w_dense):
        import jax, jax.numpy as jnp
        import numpy as np
        B, SQ, HIDDEN = (2, 512, 512)
        HEADS, GROUPS, KVC = (16, 4, 128)
        HPG = HEADS // GROUPS
        LAYER_INDEX = 1
        SCALE = KVC ** (-0.5)
        b, sq, _ = x.shape
        sk = sq
        q = jnp.einsum('bsh,he->bse', x, w_q).reshape(b, sq, GROUPS, HPG, KVC)
        kv = jnp.einsum('bsh,he->bse', x, w_kv)
        k, v = jnp.split(kv, 2, axis=-1)
        k = k.reshape(b, sk, GROUPS, KVC)
        v = v.reshape(b, sk, GROUPS, KVC)
        scores = jnp.einsum('bqgpd,bkgd->bgqpk', q, k) * (SCALE / LAYER_INDEX)
        scores = scores.astype(jnp.float32) * LAYER_INDEX
        causal = jnp.arange(sq)[:, None] >= jnp.arange(sk)[None, :]
        scores = jnp.where(causal[None, None, :, None, :], scores, -jnp.inf)
        probs = jax.nn.softmax(scores, axis=-1).astype(x.dtype)
        ctx = jnp.einsum('bgqpk,bkgd->bqgpd', probs, v).reshape(b, sq, HEADS * KVC)
        return jnp.einsum('bse,eh->bsh', ctx, w_dense)

    def _L0_ffn_ref(hidden_tensor, Wr, br, W1, W2, Ws1, Ws2):
        import jax, jax.numpy as jnp
        import numpy as np
        D = 512
        M = 256
        E = 32
        K = 6
        G = 8
        KG = 4
        SH = 512
        SCALE = 2.5

        def _route(xf, Wr, br):
            T = xf.shape[0]
            s = jax.nn.sigmoid(xf @ Wr.T + br)
            sg = s.reshape(T, G, E // G)
            group_w = jax.lax.top_k(sg, 2)[0].sum(-1)
            top_g = jax.lax.top_k(group_w, KG)[1]
            gmask = jnp.zeros((T, G), bool).at[jnp.arange(T)[:, None], top_g].set(True)
            masked = jnp.where(gmask[:, :, None], sg, 0.0).reshape(T, E)
            idx = jax.lax.top_k(masked, K)[1]
            w = jnp.take_along_axis(s, idx, axis=1)
            w = w / (w.sum(-1, keepdims=True) + 1e-20)
            return (idx, w * SCALE)
        B, Tlen, C = hidden_tensor.shape
        xf = hidden_tensor.reshape(-1, C).astype(jnp.float32)
        T = xf.shape[0]
        idx, w = _route(xf, Wr, br)
        gate = jnp.zeros((T, E), w.dtype).at[jnp.arange(T)[:, None], idx].add(w)

        def step(acc, ew):
            w1, w2, g = ew
            h = jnp.square(jax.nn.relu(xf @ w1.T)) @ w2.T
            return (acc + g[:, None] * h, None)
        acc, _ = jax.lax.scan(step, jnp.zeros_like(xf), (W1, W2, gate.T))
        moe_out = acc.reshape(B, Tlen, C).astype(hidden_tensor.dtype)
        shared = jnp.square(jax.nn.relu(hidden_tensor @ Ws1.T)) @ Ws2.T
        return shared + moe_out
    x = L0_attn_x
    xn = _layernorm(x, axis=-1)
    x = x + _L0_attn_ref(xn, L0_attn_w_q, L0_attn_w_kv, L0_attn_w_dense) + _L0_ffn_ref(xn, L0_ffn_Wr, L0_ffn_br, L0_ffn_W1, L0_ffn_W2, L0_ffn_Ws1, L0_ffn_Ws2)
    return x

_drawn_inputs = setup_inputs


def setup_inputs(seed=0):
    import zlib

    import numpy as np

    out = dict(_drawn_inputs(seed))
    spreads = {}
    factors = {'L0_attn_w_q': 7.713, 'L0_ffn_br': 3.364}
    for name, (base, spread) in spreads.items():
        noise = np.random.default_rng([zlib.crc32(name.encode()), seed]).standard_normal(out[name].shape)
        drawn = base * np.exp(spread * noise) if base else spread * noise
        out[name] = jnp.asarray(drawn.astype(out[name].dtype))
    for name, factor in factors.items():
        out[name] = (out[name] * factor).astype(out[name].dtype)
    return out
```

```python
import numpy as np

import concourse.bass as bass
from concourse import mybir
from contextlib import ExitStack

F32 = mybir.dt.float32
F32R = mybir.dt.float32r
ALU = mybir.AluOpType
ACT = mybir.ActivationFunctionType
AX = mybir.AxisListType

P = 128
B, SQ, D = 2, 1024, 512
KD = D // P
NT = SQ // P
HEADS, GROUPS, HD = 16, 4, 128
HPG = HEADS // GROUPS
SCALE = float(HD) ** -0.5
E, M = 32, 256
SH = 512
EA = E + SH // M
KM = M // P
G, EG, KG, TOPK = 8, 4, 4, 6
ROUTE_SCALE = 2.5
EPS = 1e-5
MASKED = -3.0e38

W_COLS = KD * M + KM * D
WQ_COLS, WKV_COLS, WD_COLS = KD * HPG * HD, KD * 2 * HD, HPG * D
PIECE = 1024
WA_COLS = WQ_COLS + WKV_COLS + WD_COLS
PIECES = WA_COLS // PIECE
C = 512
NC = SQ // C
UNITS = 2 * NC
PAIRS = EA // 2
TRI = NT * (NT + 1) // 2


def past(n):
    return n + 1


def stage_steps(i):
    fill = [("S", i + 1, h) for h in range(HPG)] if i + 1 < NT else []
    steps = fill[:2]
    if i >= 1:
        steps.append(("D", i - 1, 0))
    rest = fill[2:]
    for kb in range(i + 1):
        steps.append(("T", i, kb))
        if rest:
            steps.append(rest.pop(0))
        if kb >= 1:
            steps.append(("V", i, kb - 1))
    steps.append(("V", i, i))
    steps += rest
    return steps


def attention_steps():
    steps = [("Q", 0, h) for h in range(HPG)] + [("S", 0, h) for h in range(HPG)]
    for i in range(NT):
        if i + 1 == NT // 2:
            steps += [("Q", 1, h) for h in range(HPG)]
        steps += stage_steps(i)
    return steps + [("D", NT - 1, 0)]


STEPS = attention_steps()

def blocks_before(i):
    return i * (i + 1) // 2


def moe_attention_kernel(nc, x, wa, we, wr, br, out):
    xb = x.rearrange("b (t p) d -> p (b t) d", p=P)
    outb = out.rearrange("b (t p) d -> p (b t) d", p=P)

    with ExitStack() as ctx:
        def sb(name, shape, dt, stack=ctx):
            return stack.enter_context(nc.sbuf_tensor(name, shape, dt))

        def sem(name):
            return ctx.enter_context(nc.semaphore(name))

        acc = sb("acc", [P, NT, D], F32)
        xT_hi = sb("xT_hi", [P, KD, SQ], F32R)
        xT_lo = sb("xT_lo", [P, KD, SQ], F32R)
        ident = sb("ident", [P, P], F32)
        ident_r = sb("ident_r", [P, P], F32R)
        causal = sb("causal", [P, P], F32)
        causal_r = sb("causal_r", [P, P], F32R)
        wr_sb = sb("wr_sb", [P, KD, E], F32)
        br_sb = sb("br_sb", [P, E], F32)
        gate = sb("gate", [P, NT, EA], F32)
        stats = sb("stats", [P, NT, 6], F32)
        mv = sb("mv", [P, NT, 2], F32)
        std = sb("std", [P, NT], F32)
        rstd = sb("rstd", [P, NT], F32)
        xn = sb("xn", [P, 2, D], F32)
        xf = sb("xf", [P, 2, KD, P], F32)
        rz = sb("rz", [P, NT, E], F32)
        rs = sb("rs", [P, NT, E], F32)
        rhi = sb("rhi", [P, NT * G, 2], F32)
        rlo = sb("rlo", [P, NT * G, 2], F32)
        rcross = sb("rcross", [P, NT * G], F32)
        rgw = sb("rgw", [P, NT * G], F32)
        top_g = sb("top_g", [P, NT, 8], F32)
        rgm = sb("rgm", [P, NT * G], F32)
        rmask = sb("rmask", [P, NT, E], F32)
        top_e = sb("top_e", [P, NT, 8], F32)
        spare = sb("spare", [P, 1], F32)
        rsum = sb("rsum", [P, NT], F32)
        araw = sb("araw", [P, 2, PIECE], F32)

        with ExitStack() as room:
            wa_hi = sb("wa_hi", [P, WA_COLS], F32R, room)
            wa_lo = sb("wa_lo", [P, WA_COLS], F32R, room)
            qT_hi = sb("qT_hi", [P, HPG, C], F32R, room)
            qT_lo = sb("qT_lo", [P, HPG, C], F32R, room)
            kT_hi = sb("kT_hi", [P, SQ], F32R, room)
            kT_lo = sb("kT_lo", [P, SQ], F32R, room)
            vT = sb("vT", [P, NC, C], F32, room)
            v_hi = sb("v_hi", [P, NT, HD], F32R, room)
            v_lo = sb("v_lo", [P, NT, HD], F32R, room)
            probs = sb("probs", [P, 2, HPG, SQ], F32, room)
            pT_hi = sb("pT_hi", [P, 2, HPG * P], F32R, room)
            pT_lo = sb("pT_lo", [P, 2, HPG * P], F32R, room)
            cT_hi = sb("cT_hi", [P, HPG * P], F32R, room)
            cT_lo = sb("cT_lo", [P, HPG * P], F32R, room)
            negmax = sb("negmax", [P, 2, HPG], F32, room)
            rowsum = sb("rowsum", [P, 2, HPG], F32, room)
            rnorm = sb("rnorm", [P, 2, HPG], F32, room)
        with ExitStack() as room:
            eraw = sb("eraw", [P, 2, W_COLS], F32, room)
            w_hi = sb("w_hi", [P, 2, W_COLS], F32R, room)
            w_lo = sb("w_lo", [P, 2, W_COLS], F32R, room)
            relu = sb("relu", [P, 2, KM, C], F32, room)
            hsq = sb("hsq", [P, KM, C], F32, room)
            h_hi = sb("h_hi", [P, 2, KM, C], F32R, room)
            h_lo = sb("h_lo", [P, 2, KM, C], F32R, room)

        banks = [ctx.enter_context(nc.psum_tensor(f"bank{i}", [P, 512], F32)) for i in range(4, 8)]
        ps_s = ctx.enter_context(nc.psum_tensor("ps_s", [P, 4, 512], F32))
        ps_t = banks[0:2]
        ps_ctx = banks[2]
        ps_d = banks[3]
        ps_logit = banks[2]

        consts_in = sem("consts_in")
        x_in = sem("x_in")
        out_done = sem("out_done")
        pool_chain = sem("pool_chain")
        consts_ready = sem("consts_ready")
        ln_chain = sem("ln_chain")
        std_ready = sem("std_ready")
        xn_ready = sem("xn_ready")
        xnT_ready = sem("xnT_ready")
        xf_ready = sem("xf_ready")
        xhi_ready = sem("xhi_ready")
        xlo_ready = sem("xlo_ready")
        logits_ready = sem("logits_ready")
        z_ready = sem("z_ready")
        ez_ready = sem("ez_ready")
        gate_ready = sem("gate_ready")
        eraw_in = [sem("eraw_in0"), sem("eraw_in1")]
        ew_hi = sem("ew_hi")
        ew_lo = sem("ew_lo")
        h_ready = sem("h_ready")
        relu_ready = sem("relu_ready")
        hhi_ready = sem("hhi_ready")
        hsq_ready = sem("hsq_ready")
        hlo_ready = sem("hlo_ready")
        y_ready = sem("y_ready")
        y_added = sem("y_added")
        araw_in = [sem("araw_in0"), sem("araw_in1")]
        aw_hi = sem("aw_hi")
        aw_lo = sem("aw_lo")
        proj_ready = sem("proj_ready")
        proj_hi = sem("proj_hi")
        proj_lo = sem("proj_lo")
        vtr_ready = sem("vtr_ready")
        v_hi_ready = sem("v_hi_ready")
        v_lo_ready = sem("v_lo_ready")
        scores_ready = sem("scores_ready")
        max_ready = sem("max_ready")
        exp_ready = sem("exp_ready")
        rnorm_ready = sem("rnorm_ready")
        probs_ready = sem("probs_ready")
        pt_ready = sem("pt_ready")
        pt_hi_ready = sem("pt_hi_ready")
        pt_lo_ready = sem("pt_lo_ready")
        pv_done = sem("pv_done")
        ctx_hi_ready = sem("ctx_hi_ready")
        ctx_lo_ready = sem("ctx_lo_ready")
        dense_ready = sem("dense_ready")
        dense_added = sem("dense_added")

        start_at_one = (out_done, dense_added, ew_hi, ew_lo, aw_hi, aw_lo,
                        xf_ready, exp_ready, relu_ready, y_added,
                        ctx_lo_ready, logits_ready, xlo_ready, y_ready, hsq_ready, dense_ready, hlo_ready)
        started = sem("started")

        PROJ = 2 * NC + 2 * HPG
        SPLIT = PROJ - NC
        N_UNITS = NT * HPG

        wq = lambda w: w[:, 0:WQ_COLS].rearrange("p (k n) -> p k n", k=KD)
        wkv = lambda w: w[:, WQ_COLS:WQ_COLS + WKV_COLS].rearrange("p (k n) -> p k n", k=KD)
        wd = lambda w: w[:, WQ_COLS + WKV_COLS:WA_COLS].rearrange("p (h n) -> p h n", h=HPG)
        w1 = lambda w, s: w[:, s, 0:KD * M].rearrange("p (k m) -> p k m", k=KD)
        w2 = lambda w, s: w[:, s, KD * M:W_COLS].rearrange("p (k n) -> p k n", k=KM)

        def unit_of(i, h):
            return i * HPG + h

        block = ctx.enter_context(nc.Block())

        @block.sync
        def _(sp):
            sp.wait_ge(started, 4)
            sp.dma_start(wr_sb[:, :, :], wr).then_inc(consts_in, 16)
            sp.dma_start(br_sb[:, :], br).then_inc(consts_in, 16)
            with sp.Fori(0, B) as b:
                sp.wait_ge(out_done, past(b * 16))
                sp.dma_start(acc[:, :, :], xb[:, bass.ds(b * NT, NT), :]).then_inc(x_in, 16)
                with sp.Fori(0, PAIRS) as j:
                    sp.wait_ge(dense_added, past(b * (GROUPS * NT)))
                    pair = b * PAIRS + j
                    for s in range(2):
                        sp.wait_ge(ew_hi, past(pair * 2 + s - 1 if s else pair * 2))
                        sp.wait_ge(ew_lo, past(pair * 2 + s - 1 if s else pair * 2))
                        sp.dma_start(eraw[:, s, :], we[bass.ds((j * 2 + s) * P, P), :]).then_inc(eraw_in[s], 16)
                with sp.Fori(0, GROUPS) as g:
                    n = b * GROUPS + g
                    for c in range(PIECES):
                        if c >= 2:
                            sp.wait_ge(aw_hi, past(n * PIECES + c - 1))
                            sp.wait_ge(aw_lo, past(n * PIECES + c - 1))
                        else:
                            sp.wait_ge(aw_hi, past(n * PIECES))
                            sp.wait_ge(aw_lo, past(n * PIECES))
                        sp.dma_start(araw[:, c % 2, :],
                                     wa[bass.ds(g * P, P), c * PIECE:(c + 1) * PIECE]).then_inc(araw_in[c % 2], 16)
                sp.wait_ge(dense_added, past((b + 1) * (GROUPS * NT)))
                sp.dma_start(outb[:, bass.ds(b * NT, NT), :], acc[:, :, :]).then_inc(out_done, 16)
            sp.wait_ge(out_done, past(16 * B))

        @block.gpsimd
        def _(pool):
            for s in start_at_one:
                pool.sem_inc(s, 1)
            pool.sem_inc(started, 4)
            pool.memset(ident[:, :], 0.0).then_inc(pool_chain, 1)
            pool.memset(causal[:, :], 0.0).then_inc(pool_chain, 1)
            pool.memset(gate[:, :, E:EA], 1.0).then_inc(pool_chain, 1)
            pool.wait_ge(pool_chain, 3)
            pool.affine_select(out=ident[:, :], in_=ident[:, :], compare_op=ALU.not_equal, fill=1.0,
                               base=0, pattern=[[-1, P]], channel_multiplier=1).then_inc(consts_ready, 1)
            pool.affine_select(out=causal[:, :], in_=causal[:, :], compare_op=ALU.is_ge, fill=MASKED,
                               base=0, pattern=[[-1, P]], channel_multiplier=1).then_inc(consts_ready, 1)
            pool.wait_ge(consts_ready, 2)
            pool.tensor_copy(ident_r[:, :], ident[:, :]).then_inc(consts_ready, 1)
            pool.tensor_copy(causal_r[:, :], causal[:, :]).then_inc(consts_ready, 1)

        @block.tensor
        def _(pe):
            pe.wait_ge(started, 4)
            def split_product(out_, lhs, rhs, parts, n_inc, first=True, last=True):
                for k in range(parts):
                    (lh, ll), (rh, rl) = lhs(k), rhs(k)
                    pe.matmul(out_, lh, rh, start=(first and k == 0), stop=False)
                    pe.matmul(out_, lh, rl, start=False, stop=False)
                    mm = pe.matmul(out_, ll, rh, start=False, stop=(last and k == parts - 1))
                if n_inc is not None:
                    mm.then_inc(n_inc, 1)
                return mm

            pe.wait_ge(consts_ready, 4)
            pe.wait_ge(consts_in, 32)
            with pe.Fori(0, B) as b:
                with pe.Fori(0, NT // 2) as tt:
                    for s in range(2):
                        t = b * NT + tt * 2 + s
                        pe.wait_ge(xn_ready, t + 1)
                        if s == 0:
                            pe.wait_ge(xf_ready, past(t))
                        for k in range(KD):
                            mm = pe.transpose(ps_t[s][:, k * P:(k + 1) * P], xn[:, s, k * P:(k + 1) * P], ident[:, :])
                        mm.then_inc(xnT_ready, 1)
                        pe.wait_ge(xf_ready, past(t + 1))
                        for k in range(KD):
                            mm = pe.matmul(ps_logit[:, bass.ds((tt * 2 + s) * E, E)], xf[:, s, k, :], wr_sb[:, k, :],
                                           start=(k == 0), stop=(k == KD - 1))
                        mm.then_inc(logits_ready, 1)
                with pe.Fori(0, PAIRS) as j:
                    pe.wait_ge(xhi_ready, (b + 1) * NT)
                    pe.wait_ge(xlo_ready, past((b + 1) * NT))
                    pe.wait_ge(dense_added, past(b * (GROUPS * NT)))
                    pe.wait_ge(z_ready, b + 1)
                    pair = b * PAIRS + j

                    def hidden(u):
                        e, c = divmod(u, NC)
                        if c == 0:
                            pe.wait_ge(ew_hi, past(pair * 2 + e + 1))
                            pe.wait_ge(ew_lo, past(pair * 2 + e + 1))
                        if u >= 2:
                            pe.wait_ge(relu_ready, past((pair * UNITS + u - 1) * KM))
                        else:
                            pe.wait_ge(relu_ready, past(pair * UNITS * KM))
                        cs = slice(c * C, (c + 1) * C)
                        for m in range(KM):
                            ms = slice(m * P, (m + 1) * P)
                            split_product(ps_s[:, 2 * (u % 2) + m, :],
                                          lambda k: (w1(w_hi, e)[:, k, ms], w1(w_lo, e)[:, k, ms]),
                                          lambda k: (xT_hi[:, k, cs], xT_lo[:, k, cs]), KD, h_ready)

                    def outputs(u):
                        e, c = divmod(u, NC)
                        pe.wait_ge(hhi_ready, (pair * UNITS + u + 1) * KM)
                        pe.wait_ge(hlo_ready, past(pair * UNITS + u + 1))
                        for q in range(C // P):
                            pe.wait_ge(y_added, past((pair * UNITS + u) * (C // P) - (C // P - 1 - q)
                                       if u else pair * (UNITS * (C // P))))
                            qs = slice(q * P, (q + 1) * P)
                            split_product(banks[q][:, :],
                                          lambda m: (h_hi[:, u % 2, m, qs], h_lo[:, u % 2, m, qs]),
                                          lambda m: (w2(w_hi, e)[:, m, :], w2(w_lo, e)[:, m, :]), KM, y_ready)

                    hidden(0)
                    for u in range(1, UNITS):
                        hidden(u)
                        outputs(u - 1)
                    outputs(UNITS - 1)
                with pe.Fori(0, GROUPS) as g:
                    pe.wait_ge(y_added, past((b + 1) * (PAIRS * UNITS * (C // P))))
                    n = b * GROUPS + g
                    pe.wait_ge(aw_hi, past(n * PIECES + 3))
                    pe.wait_ge(aw_lo, past(n * PIECES + 3))
                    pe.wait_ge(exp_ready, past(n * N_UNITS))

                    def project(j, cols, c):
                        if j in (2, 3):
                            pe.wait_ge(proj_lo, n * SPLIT + j - 1)
                        elif j in (4, 5):
                            pe.wait_ge(proj_hi, n * PROJ + j - 1)
                        elif j >= 6:
                            pe.wait_ge(proj_lo, n * SPLIT + j - 1 - NC)
                        cs = slice(c * C, (c + 1) * C)
                        split_product(ps_s[:, 1 + 2 * (j % 2), :],
                                      lambda k: (cols(wa_hi)[k], cols(wa_lo)[k]),
                                      lambda k: (xT_hi[:, k, cs], xT_lo[:, k, cs]), KD, proj_ready)

                    for c in range(NC):
                        project(c, lambda w: [wkv(w)[:, k, 0:HD] for k in range(KD)], c)
                    for c in range(NC):
                        project(NC + c, lambda w: [wkv(w)[:, k, HD:2 * HD] for k in range(KD)], c)
                    unit = 0
                    blk = 0
                    for kind, i, a in STEPS:
                        if kind == "Q":
                            project(2 * NC + i * HPG + a,
                                    lambda w: [wq(w)[:, k, a * HD:(a + 1) * HD] for k in range(KD)], i)
                            if i == 0 and a == 1:
                                for c in range(NC):
                                    pe.wait_ge(proj_hi, n * PROJ + NC + c + 1)
                                    for q in range(C // P):
                                        mm = pe.transpose(ps_t[c][:, q * P:(q + 1) * P],
                                                          vT[:, c, q * P:(q + 1) * P], ident[:, :])
                                    mm.then_inc(vtr_ready, 1)
                        elif kind == "S":
                            if a == 0 and i in (0, NT // 2):
                                pe.wait_ge(proj_lo, n * SPLIT + NC + (i // (NT // 2) + 1) * HPG)
                            if unit >= 2:
                                pe.wait_ge(exp_ready, past(n * N_UNITS + unit - 1))
                            keys = (i + 1) * P
                            qs = slice((i % (NT // 2)) * P, (i % (NT // 2) + 1) * P)
                            for c0 in range(0, keys, 512):
                                c1 = min(c0 + 512, keys)
                                o = ps_s[:, 2 * (unit % 2) + c0 // 512, 0:c1 - c0]
                                q_h, q_l, ks = qT_hi[:, a, qs], qT_lo[:, a, qs], slice(c0, c1)
                                pe.matmul(o, q_h, kT_hi[:, ks], start=True, stop=False)
                                if c1 == keys:
                                    pe.matmul(o[:, c1 - c0 - P:c1 - c0], ident_r[:, :], causal_r[:, :],
                                              start=False, stop=False, skip_group_check=True)
                                pe.matmul(o, q_h, kT_lo[:, ks], start=False, stop=False)
                                mm = pe.matmul(o, q_l, kT_hi[:, ks], start=False, stop=True)
                            mm.then_inc(scores_ready, 1)
                            unit += 1
                        elif kind == "T":
                            pe.wait_ge(probs_ready, n * N_UNITS + (i + 1) * HPG)
                            if blk == 0:
                                pe.wait_ge(v_lo_ready, n * NC + NC)
                            if blk >= 2:
                                pe.wait_ge(pt_lo_ready, n * TRI + blk - 1)
                            for h in range(HPG):
                                mm = pe.transpose(ps_t[blk % 2][:, h * P:(h + 1) * P],
                                                  probs[:, i % 2, h, a * P:(a + 1) * P], ident[:, :])
                            mm.then_inc(pt_ready, 1)
                            blk += 1
                        elif kind == "V":
                            vb = blocks_before(i) + a
                            pe.wait_ge(pt_lo_ready, n * TRI + vb + 1)
                            if a == 0:
                                pe.wait_ge(ctx_lo_ready, past(n * NT + i))
                            split_product(ps_ctx[:, :], lambda k: (v_hi[:, a, :], v_lo[:, a, :]),
                                          lambda k: (pT_hi[:, vb % 2, :], pT_lo[:, vb % 2, :]), 1, pv_done,
                                          first=(a == 0), last=(a == i))
                        elif kind == "D":
                            if i == 0:
                                pe.wait_ge(aw_lo, past((n + 1) * PIECES))
                            pe.wait_ge(ctx_lo_ready, past(n * NT + i + 1))
                            pe.wait_ge(dense_added, past(n * NT + i))
                            split_product(ps_d[:, :],
                                          lambda h: (cT_hi[:, h * P:(h + 1) * P], cT_lo[:, h * P:(h + 1) * P]),
                                          lambda h: (wd(wa_hi)[:, h, :], wd(wa_lo)[:, h, :]), HPG, dense_ready)

        @block.scalar
        def _(act):
            act.wait_ge(started, 4)
            with act.Fori(0, B) as b:
                act.wait_ge(std_ready, b * 2 + 1)
                act.activation(std[:, :], rstd[:, :], ACT.Sqrt).then_inc(std_ready, 1)
                with act.Fori(0, NT // 2) as tt:
                    for s in range(2):
                        t = b * NT + tt * 2 + s
                        act.wait_ge(xnT_ready, t + 1)
                        if s == 0:
                            act.wait_ge(logits_ready, past(t))
                            act.wait_ge(xlo_ready, past(t))
                        act.activation(xf[:, s, :, :], ps_t[s][:, :].rearrange("p (k n) -> p k n", k=KD),
                                       ACT.Copy).then_inc(xf_ready, 1)
                        act.wait_ge(xf_ready, past(t + 1))
                        act.activation(xT_hi[:, :, bass.ds((tt * 2 + s) * P, P)], xf[:, s, :, :],
                                       ACT.Copy).then_inc(xhi_ready, 1)
                act.wait_ge(z_ready, b + 1)
                act.activation(rs[:, :, :], rz[:, :, :], ACT.Exp, scale=-1.0).then_inc(ez_ready, 1)
                with act.Fori(0, PAIRS) as j:
                    pair = b * PAIRS + j
                    for u in range(UNITS):
                        e, c = divmod(u, NC)
                        if c == 0:
                            act.wait_ge(eraw_in[e], pair * 16 + 16)
                            act.wait_ge(y_ready, past(pair * (UNITS * (C // P))))
                            act.activation(w_hi[:, e, :], eraw[:, e, :], ACT.Copy).then_inc(ew_hi, 1)
                        for m in range(KM):
                            act.wait_ge(h_ready, (pair * UNITS + u) * KM + m + 1)
                            if u >= 2:
                                act.wait_ge(hsq_ready, past(pair * UNITS + u - 1))
                            else:
                                act.wait_ge(hsq_ready, past(pair * UNITS))
                            act.activation(relu[:, u % 2, m, :], ps_s[:, 2 * (u % 2) + m, :],
                                           ACT.Relu).then_inc(relu_ready, 1)
                        if u >= 2:
                            act.wait_ge(y_ready, past((pair * UNITS + u - 1) * (C // P)))
                        else:
                            act.wait_ge(y_ready, past(pair * (UNITS * (C // P))))
                        for m in range(KM):
                            act.wait_ge(relu_ready, past((pair * UNITS + u) * KM + m + 1))
                            act.activation(h_hi[:, u % 2, m, :], relu[:, u % 2, m, :],
                                           ACT.Square).then_inc(hhi_ready, 1)
                with act.Fori(0, GROUPS) as g:
                    act.wait_ge(y_added, past((b + 1) * (PAIRS * UNITS * (C // P))))
                    n = b * GROUPS + g
                    for c in range(PIECES):
                        act.wait_ge(araw_in[c % 2], n * (16 * (PIECES - PIECES // 2 if c % 2 == 0 else PIECES // 2)) + 16 * (c // 2 + 1))
                        act.wait_ge(dense_ready, past(n * NT))
                        act.activation(wa_hi[:, c * PIECE:(c + 1) * PIECE], araw[:, c % 2, :],
                                       ACT.Copy).then_inc(aw_hi, 1)
                    for c in range(NC):
                        act.wait_ge(proj_ready, n * PROJ + c + 1)
                        act.activation(kT_hi[:, c * C:(c + 1) * C], ps_s[:, 1 + 2 * (c % 2), :],
                                       ACT.Copy).then_inc(proj_hi, 1)
                    for c in range(NC):
                        act.wait_ge(proj_ready, n * PROJ + NC + c + 1)
                        act.activation(vT[:, c, :], ps_s[:, 1 + 2 * (c % 2), :], ACT.Copy).then_inc(proj_hi, 1)
                    unit = 0
                    blk = 0
                    for kind, i, a in STEPS:
                        if kind == "Q":
                            j = 2 * NC + i * HPG + a
                            act.wait_ge(proj_ready, n * PROJ + j + 1)
                            if i:
                                act.wait_ge(scores_ready, n * N_UNITS + N_UNITS // 2)
                            act.activation(qT_hi[:, a, :], ps_s[:, 1 + 2 * (j % 2), :], ACT.Copy,
                                           scale=SCALE).then_inc(proj_hi, 1)
                            if i == 0 and a == 1:
                                for c in range(NC):
                                    act.wait_ge(vtr_ready, n * NC + c + 1)
                                    act.activation(v_hi[:, c * (C // P):(c + 1) * (C // P), :],
                                                   ps_t[c][:, :].rearrange("p (q d) -> p q d", q=C // P),
                                                   ACT.Copy).then_inc(v_hi_ready, 1)
                        elif kind == "S":
                            act.wait_ge(max_ready, n * N_UNITS + unit + 1)
                            if i >= 2:
                                act.wait_ge(pt_ready, n * TRI + blocks_before(i - 1))
                            keys = (i + 1) * P
                            s = 2 * (unit % 2)
                            src = ps_s[:, s:s + 2, :].rearrange("p c n -> p (c n)")[:, 0:keys]
                            act.activation(probs[:, i % 2, a, 0:keys], src, ACT.Exp,
                                           bias=negmax[:, i % 2, a:a + 1],
                                           accum_out=rowsum[:, i % 2, a:a + 1]).then_inc(exp_ready, 1)
                            unit += 1
                        elif kind == "T":
                            act.wait_ge(pt_ready, n * TRI + blk + 1)
                            if blk >= 2:
                                act.wait_ge(pv_done, n * TRI + blk - 1)
                            act.activation(pT_hi[:, blk % 2, :], ps_t[blk % 2][:, :], ACT.Copy).then_inc(pt_hi_ready, 1)
                            blk += 1
                        elif kind == "V" and a == i:
                            act.wait_ge(pv_done, n * TRI + blocks_before(i + 1))
                            act.wait_ge(dense_ready, past(n * NT + i))
                            act.activation(cT_hi[:, :], ps_ctx[:, :], ACT.Copy).then_inc(ctx_hi_ready, 1)

        @block.vector
        def _(dve):
            dve.wait_ge(started, 4)
            LINKS = 24

            with dve.Fori(0, B) as b:
                base = b * LINKS
                link = [0]

                def chain(ins):
                    link[0] += 1
                    ins.then_inc(ln_chain, 1)
                    dve.wait_ge(ln_chain, base + link[0])

                def hold():
                    dve.memset(spare[:, :], 0.0)

                dve.wait_ge(x_in, b * 16 + 16)
                for t in range(NT):
                    last = dve.bn_stats(stats[:, t, :], acc[:, t, :])
                chain(last)
                hold()
                for t in range(NT):
                    last = dve.bn_aggr(mv[:, t, :], stats[:, t, :])
                chain(last)
                dve.tensor_scalar(rstd[:, :], mv[:, :, 1], EPS, None, ALU.add).then_inc(std_ready, 1)
                dve.wait_ge(std_ready, b * 2 + 2)
                chain(dve.reciprocal(rstd[:, :], std[:, :]))
                for t in range(NT):
                    if t >= 2:
                        dve.wait_ge(xnT_ready, b * NT + t - 1)
                    dve.tensor_scalar(xn[:, t % 2, :], acc[:, t, :], mv[:, t, 0:1], rstd[:, t:t + 1],
                                      ALU.subtract, ALU.mult).then_inc(xn_ready, 1)
                    if t >= 1:
                        dve.wait_ge(xhi_ready, b * NT + t)
                        dve.tensor_tensor(xT_lo[:, :, (t - 1) * P:t * P], xf[:, (t - 1) % 2, :, :],
                                          xT_hi[:, :, (t - 1) * P:t * P].bitcast(F32),
                                          ALU.subtract).then_inc(xlo_ready, 1)
                dve.wait_ge(xhi_ready, b * NT + NT)
                dve.tensor_tensor(xT_lo[:, :, (NT - 1) * P:NT * P], xf[:, (NT - 1) % 2, :, :],
                                  xT_hi[:, :, (NT - 1) * P:NT * P].bitcast(F32), ALU.subtract).then_inc(xlo_ready, 1)
                dve.wait_ge(logits_ready, past(b * NT + NT))
                dve.wait_ge(consts_in, 32)
                dve.tensor_tensor(rz[:, :, :], ps_logit[:, 0:NT * E].rearrange("p (t e) -> p t e", t=NT),
                                  br_sb[:, :].unsqueeze(1).to_broadcast([P, NT, E]), ALU.add).then_inc(z_ready, 1)
                dve.wait_ge(ez_ready, b + 1)
                chain(dve.tensor_scalar(rs[:, :, :], rs[:, :, :], 1.0, None, ALU.add))
                chain(dve.reciprocal(rs[:, :, :], rs[:, :, :]))
                pairs = rs[:, :, :].rearrange("p t (g a c) -> p (t g) a c", g=G, a=2)
                chain(dve.tensor_tensor(rhi[:, :, :], pairs[:, :, :, 0], pairs[:, :, :, 1], ALU.max))
                chain(dve.tensor_tensor(rlo[:, :, :], pairs[:, :, :, 0], pairs[:, :, :, 1], ALU.min))
                chain(dve.tensor_tensor(rlo[:, :, :], rlo[:, :, :], rhi[:, :, :], ALU.add))
                chain(dve.tensor_tensor(rcross[:, :], rhi[:, :, 0], rhi[:, :, 1], ALU.add))
                chain(dve.tensor_tensor(rgw[:, :], rlo[:, :, 0], rlo[:, :, 1], ALU.max))
                chain(dve.tensor_tensor(rgw[:, :], rgw[:, :], rcross[:, :], ALU.max))
                hold()
                for t in range(NT):
                    last = dve.max(out=top_g[:, t, :], in_=rgw[:, t * G:(t + 1) * G])
                chain(last)
                chain(dve.memset(top_g[:, :, KG:8], -1.0))
                hold()
                for t in range(NT):
                    last = dve.match_replace(out=rgm[:, t * G:(t + 1) * G], in_to_replace=top_g[:, t, :],
                                             in_values=rgw[:, t * G:(t + 1) * G], imm_value=-2.0)
                chain(last)
                chain(dve.tensor_scalar(rgm[:, :], rgm[:, :], -2.0, None, ALU.is_equal))
                chain(dve.tensor_tensor(rmask[:, :, :].rearrange("p t (g c) -> p (t g) c", g=G),
                                        rs[:, :, :].rearrange("p t (g c) -> p (t g) c", g=G),
                                        rgm[:, :].unsqueeze(2).to_broadcast([P, NT * G, EG]), ALU.mult))
                hold()
                for t in range(NT):
                    last = dve.max(out=top_e[:, t, :], in_=rmask[:, t, :])
                chain(last)
                chain(dve.memset(top_e[:, :, TOPK:8], -1.0))
                hold()
                for t in range(NT):
                    last = dve.match_replace(out=rz[:, t, :], in_to_replace=top_e[:, t, :],
                                             in_values=rmask[:, t, :], imm_value=-2.0)
                chain(last)
                chain(dve.scalar_tensor_tensor(out=rz[:, :, :], in0=rz[:, :, :], scalar=-2.0, in1=rs[:, :, :],
                                               op0=ALU.is_equal, op1=ALU.mult))
                chain(dve.tensor_reduce(rsum[:, :], rz[:, :, :], AX.X, ALU.add))
                chain(dve.tensor_scalar(rsum[:, :], rsum[:, :], 1e-20, None, ALU.add))
                chain(dve.reciprocal(rsum[:, :], rsum[:, :]))
                chain(dve.scalar_tensor_tensor(out=gate[:, :, 0:E], in0=rz[:, :, :], scalar=ROUTE_SCALE,
                                               in1=rsum[:, :].unsqueeze(2).to_broadcast([P, NT, E]),
                                               op0=ALU.mult, op1=ALU.mult))
                assert link[0] == LINKS, link[0]
                hold()
                with dve.Fori(0, PAIRS) as j:
                    pair = b * PAIRS + j

                    def add_outputs(u):
                        e, c = divmod(u, NC)
                        for q in range(C // P):
                            t = c * (C // P) + q
                            k = (pair * UNITS + u) * (C // P)
                            dve.wait_ge(y_ready, past(k + q + 1))
                            dve.wait_ge(y_added, past(k + q + 1 - NT if u >= 2 else pair * (UNITS * (C // P))))
                            dve.scalar_tensor_tensor(out=acc[:, t, :], in0=banks[q][:, :],
                                                     scalar=gate[:, t, bass.ds(j * 2 + e, 1)],
                                                     in1=acc[:, t, :], op0=ALU.mult,
                                                     op1=ALU.add).then_inc(y_added, 1)

                    for u in range(UNITS):
                        e, c = divmod(u, NC)
                        if c == 0:
                            dve.wait_ge(ew_hi, past(pair * 2 + e + 1))
                            dve.tensor_tensor(w_lo[:, e, :], eraw[:, e, :], w_hi[:, e, :].bitcast(F32),
                                              ALU.subtract).then_inc(ew_lo, 1)
                        dve.wait_ge(relu_ready, past((pair * UNITS + u + 1) * KM))
                        dve.wait_ge(hlo_ready, past(pair * UNITS + u))
                        dve.tensor_tensor(hsq[:, :, :], relu[:, u % 2, :, :], relu[:, u % 2, :, :],
                                          ALU.mult).then_inc(hsq_ready, 1)
                        dve.wait_ge(hsq_ready, past(pair * UNITS + u + 1))
                        dve.wait_ge(hhi_ready, (pair * UNITS + u + 1) * KM)
                        dve.tensor_tensor(h_lo[:, u % 2, :, :], hsq[:, :, :], h_hi[:, u % 2, :, :].bitcast(F32),
                                          ALU.subtract).then_inc(hlo_ready, 1)
                        if u >= 1:
                            add_outputs(u - 1)
                    add_outputs(UNITS - 1)
                with dve.Fori(0, GROUPS) as g:
                    n = b * GROUPS + g
                    for c in range(PIECES):
                        dve.wait_ge(aw_hi, past(n * PIECES + c + 1))
                        dve.tensor_tensor(wa_lo[:, c * PIECE:(c + 1) * PIECE], araw[:, c % 2, :],
                                          wa_hi[:, c * PIECE:(c + 1) * PIECE].bitcast(F32),
                                          ALU.subtract).then_inc(aw_lo, 1)
                    for c in range(NC):
                        dve.wait_ge(proj_hi, n * PROJ + c + 1)
                        dve.tensor_tensor(kT_lo[:, c * C:(c + 1) * C], ps_s[:, 1 + 2 * (c % 2), :],
                                          kT_hi[:, c * C:(c + 1) * C].bitcast(F32), ALU.subtract).then_inc(proj_lo, 1)
                    unit = 0
                    blk = 0

                    def norm(u, i, h, wait_=True):
                        dve.wait_ge(exp_ready, past(n * N_UNITS + u + 1))
                        dve.reciprocal(rnorm[:, i % 2, h:h + 1], rowsum[:, i % 2, h:h + 1]).then_inc(rnorm_ready, 1)
                        dve.wait_ge(rnorm_ready, n * N_UNITS + u + 1)
                        pr = probs[:, i % 2, h, 0:(i + 1) * P]
                        dve.tensor_scalar(pr, pr, rnorm[:, i % 2, h:h + 1], None, ALU.mult).then_inc(probs_ready, 1)

                    pending = None
                    for kind, i, a in STEPS:
                        if kind == "Q":
                            j = 2 * NC + i * HPG + a
                            dve.wait_ge(proj_hi, n * PROJ + j + 1)
                            dve.scalar_tensor_tensor(out=qT_lo[:, a, :], in0=ps_s[:, 1 + 2 * (j % 2), :],
                                                     scalar=SCALE, in1=qT_hi[:, a, :].bitcast(F32),
                                                     op0=ALU.mult, op1=ALU.subtract).then_inc(proj_lo, 1)
                            if i == 0 and a == 1:
                                for c in range(NC):
                                    dve.wait_ge(v_hi_ready, n * NC + c + 1)
                                    vs = slice(c * (C // P), (c + 1) * (C // P))
                                    dve.tensor_tensor(v_lo[:, vs, :],
                                                      ps_t[c][:, :].rearrange("p (q d) -> p q d", q=C // P),
                                                      v_hi[:, vs, :].bitcast(F32), ALU.subtract).then_inc(v_lo_ready, 1)
                        elif kind == "S":
                            dve.wait_ge(scores_ready, n * N_UNITS + unit + 1)
                            keys = (i + 1) * P
                            s = 2 * (unit % 2)
                            src = ps_s[:, s:s + 2, :].rearrange("p c n -> p (c n)")[:, 0:keys]
                            dve.tensor_reduce(negmax[:, i % 2, a:a + 1], src, AX.X, ALU.max,
                                              negate=True).then_inc(max_ready, 1)
                            if pending:
                                norm(*pending)
                            pending = (unit, i, a)
                            unit += 1
                        elif kind == "T":
                            if pending and pending[1] == i:
                                norm(*pending)
                                pending = None
                            dve.wait_ge(pt_hi_ready, n * TRI + blk + 1)
                            dve.tensor_tensor(pT_lo[:, blk % 2, :], ps_t[blk % 2][:, :],
                                              pT_hi[:, blk % 2, :].bitcast(F32), ALU.subtract).then_inc(pt_lo_ready, 1)
                            blk += 1
                        elif kind == "V" and a == i:
                            dve.wait_ge(ctx_hi_ready, n * NT + i + 1)
                            dve.tensor_tensor(cT_lo[:, :], ps_ctx[:, :], cT_hi[:, :].bitcast(F32),
                                              ALU.subtract).then_inc(ctx_lo_ready, 1)
                        elif kind == "D":
                            if pending and pending[1] == i + 1:
                                norm(*pending)
                                pending = None
                            dve.wait_ge(dense_ready, past(n * NT + i + 1))
                            if i == 0:
                                dve.wait_ge(dense_added, past(n * NT))
                                dve.wait_ge(y_added, past((b + 1) * (PAIRS * UNITS * (C // P))))
                            dve.tensor_tensor(acc[:, i, :], acc[:, i, :], ps_d[:, :], ALU.add).then_inc(dense_added, 1)


def kernel(L0_attn_x, L0_attn_w_q, L0_attn_w_kv, L0_attn_w_dense, L0_ffn_Wr, L0_ffn_br, L0_ffn_W1, L0_ffn_W2,
           L0_ffn_Ws1, L0_ffn_Ws2):
    import concourse.bacc as bacc
    from concourse.bass_utils import run_bass_kernel_spmd

    wq = np.asarray(L0_attn_w_q).reshape(KD, P, GROUPS, HPG * HD).transpose(2, 1, 0, 3).reshape(GROUPS, P, WQ_COLS)
    wkv = np.asarray(L0_attn_w_kv).reshape(KD, P, 2, GROUPS, HD).transpose(3, 1, 0, 2, 4).reshape(GROUPS, P, WKV_COLS)
    wd = np.asarray(L0_attn_w_dense).reshape(GROUPS, HPG, P, D).transpose(0, 2, 1, 3).reshape(GROUPS, P, WD_COLS)
    wa = np.ascontiguousarray(np.concatenate([wq, wkv, wd], axis=2).reshape(GROUPS * P, WA_COLS))
    w1 = np.concatenate([np.asarray(L0_ffn_W1), np.asarray(L0_ffn_Ws1).reshape(EA - E, M, D)], axis=0)
    w1 = w1.reshape(EA, M, KD, P).transpose(0, 3, 2, 1).reshape(EA, P, KD * M)
    w2 = np.concatenate([np.asarray(L0_ffn_W2), np.asarray(L0_ffn_Ws2).reshape(D, EA - E, M).transpose(1, 0, 2)], axis=0)
    w2 = w2.reshape(EA, D, KM, P).transpose(0, 3, 2, 1).reshape(EA, P, KM * D)
    we = np.ascontiguousarray(np.concatenate([w1, w2], axis=2).reshape(EA * P, W_COLS))
    wr = np.ascontiguousarray(np.asarray(L0_ffn_Wr).reshape(E, KD, P).transpose(2, 1, 0))
    br = np.ascontiguousarray(np.broadcast_to(np.asarray(L0_ffn_br), (P, E)))
    x = np.ascontiguousarray(L0_attn_x)

    nc = bacc.Bacc("TRN2", target_bir_lowering=False, num_devices=1)
    arrays = {"x": x, "wa": wa, "we": we, "wr": wr, "br": br}
    aps = [nc.dram_tensor(k, a.shape, mybir.dt.from_np(a.dtype), kind="ExternalInput").ap() for k, a in arrays.items()]
    out = nc.dram_tensor("out", (B, SQ, D), F32, kind="ExternalOutput").ap()
    moe_attention_kernel(nc, *aps, out)
    r = run_bass_kernel_spmd(nc, [arrays], core_ids=[0])
    return r.results[0]["out"]
```

```python
import numpy as np

import concourse.bass as bass
from concourse import mybir
from contextlib import ExitStack

F32 = mybir.dt.float32
F32R = mybir.dt.float32r
I32 = mybir.dt.int32
ALU = mybir.AluOpType
ACT = mybir.ActivationFunctionType
AX = mybir.AxisListType

P = 128
B, SQ, D = 2, 1024, 512
KD = D // P
NT = SQ // P
HEADS, GROUPS, HD = 16, 4, 128
HPG = HEADS // GROUPS
SCALE = float(HD) ** -0.5
E, M = 32, 256
SH = 512
NSH = SH // M
KM = M // P
G, EG, KG, TOPK = 8, 4, 4, 6
ROUTE_SCALE = 2.5
EPS = 1e-5
MASKED = -3.0e38

W_COLS = KD * M + KM * D
WQ_COLS, WKV_COLS, WD_COLS = KD * HPG * HD, KD * 2 * HD, HPG * D
PIECE = 1024
WA_COLS = WQ_COLS + WKV_COLS + WD_COLS
PIECES = WA_COLS // PIECE
C = 512
NC = SQ // C
UNITS = NSH * NC
T = B * SQ
TILES = B * NT
ROWS = 2
PR = ROWS * P
ECAP = T // P
AHEAD = 3
SLOTS = 4
COMB = 4
PAIRS = T * TOPK // PR + E
NCOMB = TOPK * NT // GROUPS
Y_START = 1 + 3 * 16
X_START = 3
TRI = NT * (NT + 1) // 2


def past(n, start=1):
    return n + start


def stage_steps(i):
    fill = [("S", i + 1, h) for h in range(HPG)] if i + 1 < NT else []
    steps = fill[:2]
    if i >= 1:
        steps.append(("D", i - 1, 0))
    rest = fill[2:]
    for kb in range(i + 1):
        steps.append(("T", i, kb))
        if rest:
            steps.append(rest.pop(0))
        if kb >= 1:
            steps.append(("V", i, kb - 1))
    steps.append(("V", i, i))
    steps += rest
    return steps


def attention_steps():
    steps = [("Q", 0, h) for h in range(HPG)] + [("S", 0, h) for h in range(HPG)]
    for i in range(NT):
        if i + 1 == NT // 2:
            steps += [("Q", 1, h) for h in range(HPG)]
        steps += stage_steps(i)
    return steps + [("D", NT - 1, 0)]


STEPS = attention_steps()

def blocks_before(i):
    return i * (i + 1) // 2


def moe_attention_kernel(nc, x, wa, we, wr, br, out):
    xb = x.rearrange("b (t p) d -> p (b t) d", p=P)
    outb = out.rearrange("b (t p) d -> p (b t) d", p=P)

    xn_d = nc.dram_tensor("normed_tokens", (T, D), F32, kind="Internal").ap()
    z_d = nc.dram_tensor("residual_and_shared", (T, D), F32, kind="Internal").ap()
    y_d = nc.dram_tensor("expert_outputs", ((PAIRS + 1) * PR, D), F32, kind="Internal").ap()
    tok_d = nc.dram_tensor("expert_tokens", (E * T, 1), I32, kind="Internal").ap()
    xn_b = xn_d.rearrange("(t p) d -> p t d", p=P)
    z_b = z_d.rearrange("(t p) d -> p t d", p=P)
    tok_rows = tok_d.rearrange("(p n) o -> p (n o)", p=P)
    tok_b = tok_d.rearrange("(e p c) o -> p e (c o)", p=P, c=ECAP)

    with ExitStack() as ctx:
        def sb(name, shape, dt, stack=ctx):
            return stack.enter_context(nc.sbuf_tensor(name, shape, dt))

        def sem(name):
            return ctx.enter_context(nc.semaphore(name))

        acc = sb("acc", [P, NT, D], F32)
        xT_hi = sb("xT_hi", [P, KD, SQ], F32R)
        xT_lo = sb("xT_lo", [P, KD, SQ], F32R)
        ident = sb("ident", [P, P], F32)
        ident_r = sb("ident_r", [P, P], F32R)
        causal = sb("causal", [P, P], F32)
        causal_r = sb("causal_r", [P, P], F32R)
        y_rows = sb("y_rows", [P, TILES, 8], I32)
        y_gate = sb("y_gate", [P, TILES, TOPK], F32)
        tok_idx = sb("tok_idx", [P, E * ECAP + ROWS], I32)
        first_pair = sb("first_pair", [P, 2, E + 1], I32)
        comb_idx = sb("comb_idx", [P, NCOMB], I32)
        comb = sb("comb", [P, COMB, D], F32)
        araw = sb("araw", [P, 2, PIECE], F32)
        settled = sb("settled", [P, NCOMB], F32)

        with ExitStack() as room:
            eraw = sb("eraw", [P, 2, W_COLS], F32, room)
            w_hi01 = sb("w_hi01", [P, 2, W_COLS], F32R, room)
            w_lo01 = sb("w_lo01", [P, 2, W_COLS], F32R, room)
            with ExitStack() as inner:
                xn = sb("xn", [P, NT, D], F32, inner)
                xf = sb("xf", [P, 2, KD, P], F32, inner)
                relu = sb("relu", [P, 2, KM, C], F32, inner)
                hsq = sb("hsq", [P, KM, C], F32, inner)
                h_hi = sb("h_hi", [P, 2, KM, C], F32R, inner)
                h_lo = sb("h_lo", [P, 2, KM, C], F32R, inner)
                wr_sb = sb("wr_sb", [P, KD, E], F32, inner)
                br_sb = sb("br_sb", [P, E], F32, inner)
                zeros = sb("zeros", [P, T * E // P], I32, inner)
                tok_all = sb("tok_all", [P, TILES], I32, inner)
                tok_s = sb("tok_s", [P, NT], I32, inner)
                before = sb("before", [P, P], F32R, inner)
                ones = sb("ones", [P, P], F32R, inner)
                tri = sb("tri", [P, P], F32, inner)
                row_base = sb("row_base", [P, E], F32, inner)
                stats = sb("stats", [P, NT, 6], F32, inner)
                mv = sb("mv", [P, NT, 2], F32, inner)
                std = sb("std", [P, NT], F32, inner)
                rstd = sb("rstd", [P, NT], F32, inner)
                rz = sb("rz", [P, NT, E], F32, inner)
                rs = sb("rs", [P, NT, E], F32, inner)
                rhi = sb("rhi", [P, NT * G, 2], F32, inner)
                rlo = sb("rlo", [P, NT * G, 2], F32, inner)
                rcross = sb("rcross", [P, NT * G], F32, inner)
                rgw = sb("rgw", [P, NT * G], F32, inner)
                top_g = sb("top_g", [P, NT, 8], F32, inner)
                rgm = sb("rgm", [P, NT * G], F32, inner)
                rmask = sb("rmask", [P, NT, E], F32, inner)
                top_e = sb("top_e", [P, NT, 8], F32, inner)
                rsel = sb("rsel", [P, NT, E], F32R, inner)
                gate = sb("gate", [P, NT, E], F32, inner)
                rsum = sb("rsum", [P, NT], F32, inner)
                seen = sb("seen", [P, NT + 1, E], F32, inner)
                rrow = sb("rrow", [P, NT, E], F32, inner)
                top_y = sb("top_y", [P, NT, 8], F32, inner)
                match = sb("match", [P, NT, TOPK, E], F32, inner)
                yrow_s = sb("yrow_s", [P, NT, 8], I32, inner)
                bits = sb("bits", [P, 2, NT, 8], I32, inner)
                tok_pos = sb("tok_pos", [P, NT, 8], I32, inner)
                pairs_i = sb("pairs_i", [P, E], I32, inner)
                pairs_f = sb("pairs_f", [P, E], F32, inner)
                scan_ones = sb("scan_ones", [P, E], F32, inner)
                scan_f = sb("scan_f", [P, E], F32, inner)
            with ExitStack() as inner:
                w_hi23 = sb("w_hi23", [P, 2, W_COLS], F32R, inner)
                w_lo23 = sb("w_lo23", [P, 2, W_COLS], F32R, inner)
                pair_idx = sb("pair_idx", [P, 2, ROWS], I32, inner)
                xg = sb("xg", [P, 2, ROWS, D], F32, inner)
                xgT_hi = sb("xgT_hi", [P, KD, PR], F32R, inner)
                xgT_lo = sb("xgT_lo", [P, KD, PR], F32R, inner)
                mrelu = sb("mrelu", [P, KM, PR], F32, inner)
                mhsq = sb("mhsq", [P, KM, PR], F32, inner)
                mh_hi = sb("mh_hi", [P, KM, PR], F32R, inner)
                mh_lo = sb("mh_lo", [P, KM, PR], F32R, inner)
                ysb = sb("ysb", [P, 2, ROWS, D], F32, inner)
        with ExitStack() as room:
            wa_hi = sb("wa_hi", [P, WA_COLS], F32R, room)
            wa_lo = sb("wa_lo", [P, WA_COLS], F32R, room)
            qT_hi = sb("qT_hi", [P, HPG, C], F32R, room)
            qT_lo = sb("qT_lo", [P, HPG, C], F32R, room)
            kT_hi = sb("kT_hi", [P, SQ], F32R, room)
            kT_lo = sb("kT_lo", [P, SQ], F32R, room)
            vT = sb("vT", [P, NC, C], F32, room)
            v_hi = sb("v_hi", [P, NT, HD], F32R, room)
            v_lo = sb("v_lo", [P, NT, HD], F32R, room)
            probs = sb("probs", [P, 2, HPG, SQ], F32, room)
            pT_hi = sb("pT_hi", [P, 2, HPG * P], F32R, room)
            pT_lo = sb("pT_lo", [P, 2, HPG * P], F32R, room)
            cT_hi = sb("cT_hi", [P, HPG * P], F32R, room)
            cT_lo = sb("cT_lo", [P, HPG * P], F32R, room)
            negmax = sb("negmax", [P, 2, HPG], F32, room)
            rowsum = sb("rowsum", [P, 2, HPG], F32, room)
            rnorm = sb("rnorm", [P, 2, HPG], F32, room)
        xn_again = probs[:, 0, :, :].rearrange("p h n -> p (h n)").rearrange("p (t d) -> p t d", d=D)

        banks = [ctx.enter_context(nc.psum_tensor(f"bank{i}", [P, 512], F32)) for i in range(4, 8)]
        ps_s = ctx.enter_context(nc.psum_tensor("ps_s", [P, 4, 512], F32))
        ps_t = banks[0:2]
        ps_ctx = banks[2]
        ps_d = banks[3]
        ps_logit = banks[2]
        ps_rank = banks[3]
        ps_x = [ps_s[:, 2, :], ps_s[:, 3, :]]
        ps_y = banks[0:2]

        consts_in = sem("consts_in")
        x_in = sem("x_in")
        z_out = sem("z_out")
        z_in = sem("z_in")
        xn_out = sem("xn_out")
        xn_in = sem("xn_in")
        out_done = sem("out_done")
        pool_chain = sem("pool_chain")
        consts_ready = sem("consts_ready")
        tok_zeroed = sem("tok_zeroed")
        ln_chain = sem("ln_chain")
        std_ready = sem("std_ready")
        xn_ready = sem("xn_ready")
        xnT_ready = sem("xnT_ready")
        xf_ready = sem("xf_ready")
        xhi_ready = sem("xhi_ready")
        xlo_ready = sem("xlo_ready")
        logits_ready = sem("logits_ready")
        z_ready = sem("z_ready")
        ez_ready = sem("ez_ready")
        sel_ready = sem("sel_ready")
        ranks_ready = sem("ranks_ready")
        ranks_read = sem("ranks_read")
        tok_pos_ready = sem("tok_pos_ready")
        tok_copied = sem("tok_copied")
        tok_out = sem("tok_out")
        tok_in = sem("tok_in")
        pairs_ready = sem("pairs_ready")
        y_rows_ready = sem("y_rows_ready")
        eraw_in = [sem("eraw_in0"), sem("eraw_in1")]
        ew_hi = sem("ew_hi")
        ew_lo = sem("ew_lo")
        h_ready = sem("h_ready")
        relu_ready = sem("relu_ready")
        hhi_ready = sem("hhi_ready")
        hsq_ready = sem("hsq_ready")
        hlo_ready = sem("hlo_ready")
        y_ready = sem("y_ready")
        y_added = sem("y_added")
        idx_ready = sem("idx_ready")
        xg_in = [sem("xg_in0"), sem("xg_in1")]
        mx_ready = sem("mx_ready")
        mx_hi = sem("mx_hi")
        mx_lo = sem("mx_lo")
        mh_ready = sem("mh_ready")
        mrelu_ready = sem("mrelu_ready")
        mhsq_ready = sem("mhsq_ready")
        mhhi_ready = sem("mhhi_ready")
        mhlo_ready = sem("mhlo_ready")
        my_ready = sem("my_ready")
        y0_copied = sem("y0_copied")
        y1_copied = sem("y1_copied")
        y_stored = sem("y_stored")
        xr_ready = sem("xr_ready")
        xr_hi = sem("xr_hi")
        xr_lo = sem("xr_lo")
        comb_idx_ready = sem("comb_idx_ready")
        comb_in = [sem(f"comb_in{i}") for i in range(COMB)]
        comb_added = sem("comb_added")
        araw_in = [sem("araw_in0"), sem("araw_in1")]
        aw_hi = sem("aw_hi")
        aw_lo = sem("aw_lo")
        proj_ready = sem("proj_ready")
        proj_hi = sem("proj_hi")
        proj_lo = sem("proj_lo")
        vtr_ready = sem("vtr_ready")
        v_hi_ready = sem("v_hi_ready")
        v_lo_ready = sem("v_lo_ready")
        scores_ready = sem("scores_ready")
        max_ready = sem("max_ready")
        exp_ready = sem("exp_ready")
        rnorm_ready = sem("rnorm_ready")
        probs_ready = sem("probs_ready")
        pt_ready = sem("pt_ready")
        pt_hi_ready = sem("pt_hi_ready")
        pt_lo_ready = sem("pt_lo_ready")
        pv_done = sem("pv_done")
        ctx_hi_ready = sem("ctx_hi_ready")
        ctx_lo_ready = sem("ctx_lo_ready")
        dense_ready = sem("dense_ready")
        dense_added = sem("dense_added")
        start_at_one = (z_out, out_done, xf_ready, logits_ready, xlo_ready, relu_ready, hsq_ready, hlo_ready,
                        y_ready, y_added, tok_copied, mrelu_ready, mhsq_ready, mhlo_ready, my_ready,
                        y0_copied, y1_copied, xr_hi, xr_lo, comb_added, aw_hi, aw_lo, exp_ready, ctx_lo_ready,
                        dense_ready, dense_added)
        started = sem("started")

        PROJ = 2 * NC + 2 * HPG
        SPLIT = PROJ - NC
        N_UNITS = NT * HPG
        CQ = C // P
        YA = UNITS * CQ
        SCATTERS = TOPK * NT
        ALL_IN = [16 * ((E + AHEAD + NSH + 1) // 2), 16 * ((E + AHEAD + NSH) // 2)]

        wq = lambda w: w[:, 0:WQ_COLS].rearrange("p (k n) -> p k n", k=KD)
        wkv = lambda w: w[:, WQ_COLS:WQ_COLS + WKV_COLS].rearrange("p (k n) -> p k n", k=KD)
        wd = lambda w: w[:, WQ_COLS + WKV_COLS:WA_COLS].rearrange("p (h n) -> p h n", h=HPG)
        w1 = lambda w: w[:, 0:KD * M].rearrange("p (k m) -> p k m", k=KD)
        w2 = lambda w: w[:, KD * M:W_COLS].rearrange("p (k n) -> p k n", k=KM)
        hi_slot = lambda s: (w_hi01, w_hi23)[s // 2][:, s % 2, :]
        lo_slot = lambda s: (w_lo01, w_lo23)[s // 2][:, s % 2, :]

        def pair_bound(eng, e, row=0):
            return eng.value_load(first_pair[0:1, row, bass.ds(e, 1)], min_val=0, max_val=PAIRS + row)

        def over_experts(eng, body, row=0):
            with eng.Fori(0, E // SLOTS) as es:
                lo = pair_bound(eng, es * SLOTS, row)
                for s in range(SLOTS):
                    hi = pair_bound(eng, es * SLOTS + s + 1, row)
                    body(es * SLOTS + s, s, lo, hi, es)
                    lo = hi

        def settle(pool, c=0):
            pool.tensor_tensor(settled[:, c:c + 1], ident[:, 0:1], ident[:, 0:1], ALU.mult)

        block = ctx.enter_context(nc.Block())

        @block.sync
        def _(sp):
            sp.wait_ge(started, 4)
            for b in range(NSH):
                sp.dma_start(eraw[:, b, :], we[(E + b) * P:(E + b + 1) * P, :]).then_inc(eraw_in[b], 16)
            sp.dma_start(wr_sb[:, :, :], wr).then_inc(consts_in, 16)
            sp.dma_start(br_sb[:, :], br).then_inc(consts_in, 16)
            sp.wait_ge(consts_ready, 4)
            sp.dma_start(tok_rows, zeros[:, :]).then_inc(tok_zeroed, 16)
            with sp.Fori(0, B) as b:
                sp.wait_ge(z_out, past(b * 16))
                sp.dma_start(acc[:, :, :], xb[:, bass.ds(b * NT, NT), :]).then_inc(x_in, 16)
                sp.wait_ge(xn_ready, (b + 1) * NT)
                sp.dma_start(xn_b[:, bass.ds(b * NT, NT), :], xn[:, :, :]).then_inc(xn_out, 16)
                sp.wait_ge(y_added, past((b + 1) * YA))
                sp.dma_start(z_b[:, bass.ds(b * NT, NT), :], acc[:, :, :]).then_inc(z_out, 16)
            sp.wait_ge(pairs_ready, 1)
            for e in range(AHEAD):
                if e >= 2:
                    sp.wait_ge(ew_lo, NSH + e - 1)
                sp.dma_start(eraw[:, e % 2, :], we[e * P:(e + 1) * P, :]).then_inc(eraw_in[e % 2], 16)
                if e == 1:
                    sp.wait_ge(tok_out, B * SCATTERS * 16)
                    sp.dma_start(tok_idx[:, 0:E * ECAP].rearrange("p (e c) -> p e c", e=E), tok_b).then_inc(tok_in, 16)

            def store_pairs(e, s, lo, hi, es):
                sp.wait_ge(ew_lo, e + (NSH + 2))
                sp.dma_start(eraw[:, (s + AHEAD) % 2, :],
                             we[bass.ds((e + AHEAD) * P, P), :]).then_inc(eraw_in[(s + AHEAD) % 2], 16)
                with sp.Fori(lo, hi) as p:
                    sp.wait_ge(y0_copied, past(p + 2))
                    sp.wait_ge(y1_copied, past(p + 2))
                    sp.wait_ge(y_stored, past(p * 16, Y_START))
                    sp.dma_start(y_d[bass.ds(p * PR, PR), :].rearrange("(r p) d -> p r d", p=P),
                                 ysb[:, bass.ds(p % 2, 1), :, :].rearrange("p s r d -> p (s r) d")).then_inc(y_stored, 16)

            over_experts(sp, store_pairs)
            last = pair_bound(sp, E)
            with sp.Fori(last, PAIRS + 1) as p:
                sp.wait_ge(y_stored, past(p * 16, Y_START))
                sp.dma_start(y_d[bass.ds(p * PR, PR), :].rearrange("(r p) d -> p r d", p=P),
                             ysb[:, 0, :, :]).then_inc(y_stored, 16)
            with sp.Fori(0, B) as b:
                sp.wait_ge(mx_lo, (last + 1) * ROWS)
                sp.wait_ge(y_stored, past((PAIRS + 1) * 16, Y_START))
                sp.wait_ge(ew_lo, NSH + E + 2)
                for s in range(2):
                    sp.wait_ge(eraw_in[s], ALL_IN[s])
                sp.wait_ge(out_done, past(b * 16))
                sp.dma_start(xn_again, xn_b[:, bass.ds(b * NT, NT), :]).then_inc(xn_in, 16)
                sp.dma_start(acc[:, :, :], z_b[:, bass.ds(b * NT, NT), :]).then_inc(z_in, 16)
                with sp.Fori(0, GROUPS) as g:
                    n = b * GROUPS + g
                    for c in range(PIECES):
                        sp.wait_ge(aw_hi, past(n * PIECES + max(c - 1, 0)))
                        sp.wait_ge(aw_lo, past(n * PIECES + max(c - 1, 0)))
                        sp.dma_start(araw[:, c % 2, :],
                                     wa[bass.ds(g * P, P), c * PIECE:(c + 1) * PIECE]).then_inc(araw_in[c % 2], 16)
                sp.wait_ge(dense_added, past((b + 1) * (GROUPS * NT)))
                sp.wait_ge(comb_added, past((b + 1) * (GROUPS * NCOMB)))
                sp.dma_start(outb[:, bass.ds(b * NT, NT), :], acc[:, :, :]).then_inc(out_done, 16)
            sp.wait_ge(out_done, past(16 * B))
            sp.wait_ge(z_out, past(16 * B))
            sp.wait_ge(xn_out, 16 * B)
            sp.wait_ge(tok_zeroed, 16)

        @block.gpsimd
        def _(pool):
            for s in start_at_one:
                pool.sem_inc(s, 1)
            pool.sem_inc(y_stored, Y_START)
            pool.sem_inc(mx_ready, X_START)
            pool.sem_inc(started, 4)
            pool.memset(ident[:, :], 0.0).then_inc(pool_chain, 1)
            pool.memset(causal[:, :], 0.0).then_inc(pool_chain, 1)
            pool.memset(tri[:, :], 1.0).then_inc(pool_chain, 1)
            pool.memset(tok_idx[:, E * ECAP:], 0).then_inc(pool_chain, 1)
            pool.iota(pairs_i[:, :], pattern=[[ECAP * P, E]], base=1, channel_multiplier=0).then_inc(pool_chain, 1)
            pool.iota(tok_all[:, :], pattern=[[P, TILES]], base=0, channel_multiplier=1).then_inc(pool_chain, 1)
            pool.wait_ge(pool_chain, 6)
            pool.affine_select(out=ident[:, :], in_=ident[:, :], compare_op=ALU.not_equal, fill=1.0,
                               base=0, pattern=[[-1, P]], channel_multiplier=1).then_inc(consts_ready, 1)
            pool.affine_select(out=causal[:, :], in_=causal[:, :], compare_op=ALU.is_ge, fill=MASKED,
                               base=0, pattern=[[-1, P]], channel_multiplier=1).then_inc(consts_ready, 1)
            pool.affine_select(out=tri[:, :], in_=tri[:, :], compare_op=ALU.is_gt, fill=0.0,
                               base=0, pattern=[[1, P]], channel_multiplier=-1).then_inc(consts_ready, 1)
            pool.memset(zeros[:, :], 0).then_inc(consts_ready, 1)
            pool.wait_ge(consts_ready, 4)
            pool.tensor_copy(ident_r[:, :], ident[:, :]).then_inc(consts_ready, 1)
            pool.tensor_copy(causal_r[:, :], causal[:, :]).then_inc(consts_ready, 1)
            pool.tensor_copy(before[:, :], tri[:, :]).then_inc(consts_ready, 1)
            pool.memset(ones[:, :].bitcast(F32), 1.0).then_inc(consts_ready, 1)
            pool.memset(scan_ones[:, :], 1.0).then_inc(consts_ready, 1)
            pool.memset(seen[:, 0, :], 0.0).then_inc(consts_ready, 1)
            pool.tensor_copy(row_base[:, :], pairs_i[:, :]).then_inc(consts_ready, 1)
            pool.wait_ge(tok_zeroed, 16)
            with pool.Fori(0, B) as b:
                pool.tensor_copy(tok_s[:, :], tok_all[:, bass.ds(b * NT, NT)]).then_inc(tok_copied, 1)
                pool.wait_ge(tok_copied, past(b + 1))
                pool.wait_ge(tok_pos_ready, b + 1)
                settle(pool)
                for t in range(NT):
                    for k in range(TOPK):
                        pool.indirect_dma_start(
                            out=tok_d, out_offset=bass.IndirectOffsetOnAxis(ap=tok_pos[:, t, k:k + 1], axis=0),
                            in_=tok_s[:, t:t + 1], in_offset=None).then_inc(tok_out, 16)
                pool.wait_ge(tok_out, (b + 1) * (SCATTERS * 16))
            pool.wait_ge(pairs_ready, 1)
            pool.wait_ge(tok_in, 16)

            def gather_pairs(e, s, lo, hi, es):
                with pool.Fori(lo, hi) as p:
                    pool.wait_ge(mx_ready, p * ROWS + (X_START - ROWS))
                    col = nc.s_assert_within(e * ECAP + (p - lo) * ROWS, 0, E * ECAP,
                                             skip_runtime_bounds_check_because="an expert has at most T tokens")
                    for slot in range(2):
                        with pool.If(p % 2 == slot):
                            pool.tensor_copy(pair_idx[:, slot, :], tok_idx[:, bass.ds(col, ROWS)]).then_inc(idx_ready, 1)
                            pool.wait_ge(idx_ready, p + 1)
                            settle(pool)
                            for r in range(ROWS):
                                pool.indirect_dma_start(
                                    out=xg[:, slot, r, :], out_offset=None, in_=xn_d,
                                    in_offset=bass.IndirectOffsetOnAxis(ap=pair_idx[:, slot, r:r + 1], axis=0)
                                ).then_inc(xg_in[slot], 16)

            over_experts(pool, gather_pairs, row=1)
            with pool.Fori(0, B) as b:
                with pool.Fori(0, GROUPS) as g:
                    n = b * GROUPS + g
                    pool.wait_ge(y_stored, past((PAIRS + 1) * 16, Y_START))
                    pool.wait_ge(y_rows_ready, 1)
                    pool.wait_ge(comb_added, past(n * NCOMB))
                    tiles = NT // GROUPS
                    src = y_rows[:, bass.ds(b * NT + g * tiles, tiles), 0:TOPK]
                    pool.tensor_copy(comb_idx[:, :].rearrange("p (t k) -> p t k", k=TOPK), src).then_inc(comb_idx_ready, 1)
                    pool.wait_ge(comb_idx_ready, n + 1)
                    settle(pool)
                    for j in range(NCOMB):
                        if j >= COMB:
                            pool.wait_ge(comb_added, past(n * NCOMB + j - COMB + 1))
                            settle(pool, j)
                        pool.indirect_dma_start(
                            out=comb[:, j % COMB, :], out_offset=None, in_=y_d,
                            in_offset=bass.IndirectOffsetOnAxis(ap=comb_idx[:, j:j + 1], axis=0)
                        ).then_inc(comb_in[j % COMB], 16)

        @block.tensor
        def _(pe):
            pe.wait_ge(started, 4)

            def split_product(out_, lhs, rhs, parts, n_inc, first=True, last=True):
                for k in range(parts):
                    (lh, ll), (rh, rl) = lhs(k), rhs(k)
                    pe.matmul(out_, lh, rh, start=(first and k == 0), stop=False)
                    pe.matmul(out_, lh, rl, start=False, stop=False)
                    mm = pe.matmul(out_, ll, rh, start=False, stop=(last and k == parts - 1))
                if n_inc is not None:
                    mm.then_inc(n_inc, 1)
                return mm

            pe.wait_ge(consts_ready, 11)
            pe.wait_ge(consts_in, 32)
            with pe.Fori(0, B) as b:
                for t in range(NT):
                    s = t % 2
                    pe.wait_ge(xn_ready, b * NT + t + 1)
                    if t == 0:
                        pe.wait_ge(y_added, past(b * YA))
                    for k in range(KD):
                        mm = pe.transpose(ps_t[s][:, k * P:(k + 1) * P], xn[:, t, k * P:(k + 1) * P], ident[:, :])
                    mm.then_inc(xnT_ready, 1)
                    pe.wait_ge(xf_ready, past(b * NT + t + 1))
                    for k in range(KD):
                        mm = pe.matmul(ps_logit[:, t * E:(t + 1) * E], xf[:, s, k, :], wr_sb[:, k, :],
                                       start=(k == 0), stop=(k == KD - 1))
                    mm.then_inc(logits_ready, 1)
                pe.wait_ge(xhi_ready, (b + 1) * NT)
                pe.wait_ge(xlo_ready, past((b + 1) * NT))
                pe.wait_ge(ew_lo, NSH)

                def hidden(u):
                    e, c = divmod(u, NC)
                    pe.wait_ge(relu_ready, past((b * UNITS + (u - 1 if u >= 2 else 0)) * KM))
                    cs = slice(c * C, (c + 1) * C)
                    for m in range(KM):
                        ms = slice(m * P, (m + 1) * P)
                        split_product(ps_s[:, 2 * (u % 2) + m, :],
                                      lambda k: (w1(hi_slot(e))[:, k, ms], w1(lo_slot(e))[:, k, ms]),
                                      lambda k: (xT_hi[:, k, cs], xT_lo[:, k, cs]), KD, h_ready)

                def outputs(u):
                    e, c = divmod(u, NC)
                    pe.wait_ge(hhi_ready, (b * UNITS + u + 1) * KM)
                    pe.wait_ge(hlo_ready, past(b * UNITS + u + 1))
                    if u == 0:
                        pe.wait_ge(z_ready, b + 1)
                        pe.wait_ge(ranks_read, b + 1)
                    for q in range(CQ):
                        if u:
                            pe.wait_ge(y_added, past((b * UNITS + u) * CQ - (CQ - 1 - q)))
                        qs = slice(q * P, (q + 1) * P)
                        split_product(banks[q][:, :],
                                      lambda m: (h_hi[:, u % 2, m, qs], h_lo[:, u % 2, m, qs]),
                                      lambda m: (w2(hi_slot(e))[:, m, :], w2(lo_slot(e))[:, m, :]), KM, y_ready)

                hidden(0)
                pe.wait_ge(sel_ready, b + 1)
                rsel_all = rsel[:, :, :].rearrange("p t e -> p (t e)")
                pe.matmul(ps_rank[:, 0:NT * E], before[:, :], rsel_all, start=True, stop=True)
                pe.matmul(ps_rank[:, NT * E:2 * NT * E], ones[:, :], rsel_all, start=True, stop=True).then_inc(ranks_ready, 1)
                for u in range(1, UNITS):
                    hidden(u)
                    outputs(u - 1)
                outputs(UNITS - 1)

            def transpose_pair(q):
                pe.wait_ge(mx_lo, q * ROWS)
                for slot in range(2):
                    with pe.If(q % 2 == slot):
                        pe.wait_ge(xg_in[slot], (q // 2 + 1) * (ROWS * 16))
                        for r in range(ROWS):
                            for k in range(KD):
                                mm = pe.transpose(ps_x[r][:, k * P:(k + 1) * P], xg[:, slot, r, k * P:(k + 1) * P],
                                                  ident[:, :])
                            mm.then_inc(mx_ready, 1)

            pe.wait_ge(pairs_ready, 1)
            pe.wait_ge(xg_in[0], ROWS * 16)
            for r in range(ROWS):
                for k in range(KD):
                    mm = pe.transpose(ps_x[r][:, k * P:(k + 1) * P], xg[:, 0, r, k * P:(k + 1) * P], ident[:, :])
                mm.then_inc(mx_ready, 1)

            def expert_pairs(e, s, lo, hi, es):
                w_hi, w_lo = hi_slot(s), lo_slot(s)
                with pe.Fori(lo, hi) as p:
                    pe.wait_ge(ew_lo, e + (NSH + 1))
                    pe.wait_ge(mx_lo, (p + 1) * ROWS)
                    pe.wait_ge(mrelu_ready, past(p * KM))
                    for m in range(KM):
                        ms = slice(m * P, (m + 1) * P)
                        split_product(ps_s[:, m, 0:PR],
                                      lambda k: (w1(w_hi)[:, k, ms], w1(w_lo)[:, k, ms]),
                                      lambda k: (xgT_hi[:, k, :], xgT_lo[:, k, :]), KD, mh_ready)
                    transpose_pair(p + 1)
                    pe.wait_ge(y0_copied, past(p + 1))
                    pe.wait_ge(y1_copied, past(p + 1))
                    for m in range(KM):
                        pe.wait_ge(mhlo_ready, past(p * KM + m + 1))
                        for r in range(ROWS):
                            rs_ = slice(r * P, (r + 1) * P)
                            split_product(ps_y[r][:, :], lambda _: (mh_hi[:, m, rs_], mh_lo[:, m, rs_]),
                                          lambda _: (w2(w_hi)[:, m, :], w2(w_lo)[:, m, :]), 1,
                                          my_ready if m == KM - 1 else None, first=(m == 0), last=(m == KM - 1))

            over_experts(pe, expert_pairs)
            with pe.Fori(0, B) as b:
                pe.wait_ge(xn_in, (b + 1) * 16)
                for t in range(NT):
                    if t >= 2:
                        pe.wait_ge(xr_lo, past(b * NT + t - 1))
                    for k in range(KD):
                        mm = pe.transpose(ps_t[t % 2][:, k * P:(k + 1) * P], xn_again[:, t, k * P:(k + 1) * P],
                                          ident[:, :])
                    mm.then_inc(xr_ready, 1)
                with pe.Fori(0, GROUPS) as g:
                    n = b * GROUPS + g
                    pe.wait_ge(xr_lo, past((b + 1) * NT))
                    pe.wait_ge(aw_hi, past(n * PIECES + 3))
                    pe.wait_ge(aw_lo, past(n * PIECES + 3))
                    pe.wait_ge(exp_ready, past(n * N_UNITS))

                    def project(j, cols, c):
                        if j in (2, 3):
                            pe.wait_ge(proj_lo, n * SPLIT + j - 1)
                        elif j in (4, 5):
                            pe.wait_ge(proj_hi, n * PROJ + j - 1)
                        elif j >= 6:
                            pe.wait_ge(proj_lo, n * SPLIT + j - 1 - NC)
                        cs = slice(c * C, (c + 1) * C)
                        split_product(ps_s[:, 1 + 2 * (j % 2), :],
                                      lambda k: (cols(wa_hi)[k], cols(wa_lo)[k]),
                                      lambda k: (xT_hi[:, k, cs], xT_lo[:, k, cs]), KD, proj_ready)

                    for c in range(NC):
                        project(c, lambda w: [wkv(w)[:, k, 0:HD] for k in range(KD)], c)
                    for c in range(NC):
                        project(NC + c, lambda w: [wkv(w)[:, k, HD:2 * HD] for k in range(KD)], c)
                    unit = 0
                    blk = 0
                    for kind, i, a in STEPS:
                        if kind == "Q":
                            project(2 * NC + i * HPG + a,
                                    lambda w: [wq(w)[:, k, a * HD:(a + 1) * HD] for k in range(KD)], i)
                            if i == 0 and a == 1:
                                for c in range(NC):
                                    pe.wait_ge(proj_hi, n * PROJ + NC + c + 1)
                                    for q in range(C // P):
                                        mm = pe.transpose(ps_t[c][:, q * P:(q + 1) * P],
                                                          vT[:, c, q * P:(q + 1) * P], ident[:, :])
                                    mm.then_inc(vtr_ready, 1)
                        elif kind == "S":
                            if a == 0 and i in (0, NT // 2):
                                pe.wait_ge(proj_lo, n * SPLIT + NC + (i // (NT // 2) + 1) * HPG)
                            if unit >= 2:
                                pe.wait_ge(exp_ready, past(n * N_UNITS + unit - 1))
                            keys = (i + 1) * P
                            qs = slice((i % (NT // 2)) * P, (i % (NT // 2) + 1) * P)
                            for c0 in range(0, keys, 512):
                                c1 = min(c0 + 512, keys)
                                o = ps_s[:, 2 * (unit % 2) + c0 // 512, 0:c1 - c0]
                                q_h, q_l, ks = qT_hi[:, a, qs], qT_lo[:, a, qs], slice(c0, c1)
                                pe.matmul(o, q_h, kT_hi[:, ks], start=True, stop=False)
                                if c1 == keys:
                                    pe.matmul(o[:, c1 - c0 - P:c1 - c0], ident_r[:, :], causal_r[:, :],
                                              start=False, stop=False, skip_group_check=True)
                                pe.matmul(o, q_h, kT_lo[:, ks], start=False, stop=False)
                                mm = pe.matmul(o, q_l, kT_hi[:, ks], start=False, stop=True)
                            mm.then_inc(scores_ready, 1)
                            unit += 1
                        elif kind == "T":
                            pe.wait_ge(probs_ready, n * N_UNITS + (i + 1) * HPG)
                            if blk == 0:
                                pe.wait_ge(v_lo_ready, n * NC + NC)
                            if blk >= 2:
                                pe.wait_ge(pt_lo_ready, n * TRI + blk - 1)
                            for h in range(HPG):
                                mm = pe.transpose(ps_t[blk % 2][:, h * P:(h + 1) * P],
                                                  probs[:, i % 2, h, a * P:(a + 1) * P], ident[:, :])
                            mm.then_inc(pt_ready, 1)
                            blk += 1
                        elif kind == "V":
                            vb = blocks_before(i) + a
                            pe.wait_ge(pt_lo_ready, n * TRI + vb + 1)
                            if a == 0:
                                pe.wait_ge(ctx_lo_ready, past(n * NT + i))
                            split_product(ps_ctx[:, :], lambda k: (v_hi[:, a, :], v_lo[:, a, :]),
                                          lambda k: (pT_hi[:, vb % 2, :], pT_lo[:, vb % 2, :]), 1, pv_done,
                                          first=(a == 0), last=(a == i))
                        elif kind == "D":
                            if i == 0:
                                pe.wait_ge(aw_lo, past((n + 1) * PIECES))
                            pe.wait_ge(ctx_lo_ready, past(n * NT + i + 1))
                            pe.wait_ge(dense_added, past(n * NT + i))
                            split_product(ps_d[:, :],
                                          lambda h: (cT_hi[:, h * P:(h + 1) * P], cT_lo[:, h * P:(h + 1) * P]),
                                          lambda h: (wd(wa_hi)[:, h, :], wd(wa_lo)[:, h, :]), HPG, dense_ready)

        @block.scalar
        def _(act):
            act.wait_ge(started, 4)
            for e in range(NSH):
                act.wait_ge(eraw_in[e], 16)
                act.activation(hi_slot(e), eraw[:, e, :], ACT.Copy).then_inc(ew_hi, 1)
            with act.Fori(0, B) as b:
                act.wait_ge(std_ready, b * 2 + 1)
                act.activation(std[:, :], rstd[:, :], ACT.Sqrt).then_inc(std_ready, 1)
                for t in range(NT):
                    s = t % 2
                    act.wait_ge(xnT_ready, b * NT + t + 1)
                    act.wait_ge(logits_ready, past(b * NT + max(t - 1, 0)))
                    act.wait_ge(xlo_ready, past(b * NT + max(t - 1, 0)))
                    act.activation(xf[:, s, :, :], ps_t[s][:, :].rearrange("p (k n) -> p k n", k=KD),
                                   ACT.Copy).then_inc(xf_ready, 1)
                    act.wait_ge(xf_ready, past(b * NT + t + 1))
                    act.activation(xT_hi[:, :, t * P:(t + 1) * P], xf[:, s, :, :], ACT.Copy).then_inc(xhi_ready, 1)
                act.wait_ge(z_ready, b + 1)
                act.activation(rs[:, :, :], rz[:, :, :], ACT.Exp, scale=-1.0).then_inc(ez_ready, 1)
                for u in range(UNITS):
                    for m in range(KM):
                        act.wait_ge(h_ready, (b * UNITS + u) * KM + m + 1)
                        act.wait_ge(hsq_ready, past(b * UNITS + (u - 1 if u >= 2 else 0)))
                        act.activation(relu[:, u % 2, m, :], ps_s[:, 2 * (u % 2) + m, :], ACT.Relu).then_inc(relu_ready, 1)
                    act.wait_ge(y_ready, past((b * UNITS + (u - 1 if u >= 2 else 0)) * CQ))
                    for m in range(KM):
                        act.wait_ge(relu_ready, past((b * UNITS + u) * KM + m + 1))
                        act.activation(h_hi[:, u % 2, m, :], relu[:, u % 2, m, :], ACT.Square).then_inc(hhi_ready, 1)

            act.wait_ge(pairs_ready, 1)
            act.wait_ge(xn_out, 16 * B)

            def upper_tokens(q):
                for r in range(ROWS):
                    act.wait_ge(mx_ready, q * ROWS + (r + 1 + X_START))
                    act.activation(xgT_hi[:, :, r * P:(r + 1) * P], ps_x[r].rearrange("p (k n) -> p k n", k=KD),
                                   ACT.Copy).then_inc(mx_hi, 1)

            def upper_weights(e, slot, es=None):
                n_in = (slot // 2 + NSH // 2 + 1) * 16 if es is None else None
                act.wait_ge(eraw_in[slot % 2], n_in if es is None else (e // 2 + (NSH // 2 + 1)) * 16)
                act.activation(hi_slot(slot), eraw[:, slot % 2, :], ACT.Copy).then_inc(ew_hi, 1)

            def copy_output(q):
                act.wait_ge(my_ready, past(q * ROWS))
                act.wait_ge(y_stored, past((q - 2) * 16, Y_START))
                act.activation(ysb[:, bass.ds((q + 1) % 2, 1), 1, :].rearrange("p s d -> p (s d)"), ps_y[1][:, :],
                               ACT.Copy).then_inc(y1_copied, 1)

            upper_weights(0, 0)
            upper_weights(1, 1)
            upper_tokens(0)

            def expert_uppers(e, s, lo, hi, es):
                upper_weights(e + 2, (s + 2) % SLOTS, es)
                with act.Fori(lo, hi) as p:
                    copy_output(p)
                    for m in range(KM):
                        act.wait_ge(mh_ready, p * KM + m + 1)
                        act.wait_ge(mhsq_ready, past(p * KM))
                        act.activation(mrelu[:, m, :], ps_s[:, m, 0:PR], ACT.Relu).then_inc(mrelu_ready, 1)
                        act.wait_ge(mrelu_ready, past(p * KM + m + 1))
                        act.activation(mh_hi[:, m, :], mrelu[:, m, :], ACT.Square).then_inc(mhhi_ready, 1)
                    upper_tokens(p + 1)

            over_experts(act, expert_uppers)
            copy_output(pair_bound(act, E))
            with act.Fori(0, B) as b:
                for t in range(NT):
                    act.wait_ge(xr_ready, b * NT + t + 1)
                    act.activation(xT_hi[:, :, t * P:(t + 1) * P], ps_t[t % 2][:, :].rearrange("p (k n) -> p k n", k=KD),
                                   ACT.Copy).then_inc(xr_hi, 1)
                with act.Fori(0, GROUPS) as g:
                    n = b * GROUPS + g
                    for c in range(PIECES):
                        act.wait_ge(araw_in[c % 2], n * (16 * (PIECES - PIECES // 2 if c % 2 == 0 else PIECES // 2)) + 16 * (c // 2 + 1))
                        act.wait_ge(dense_ready, past(n * NT))
                        act.activation(wa_hi[:, c * PIECE:(c + 1) * PIECE], araw[:, c % 2, :],
                                       ACT.Copy).then_inc(aw_hi, 1)
                    for c in range(NC):
                        act.wait_ge(proj_ready, n * PROJ + c + 1)
                        act.activation(kT_hi[:, c * C:(c + 1) * C], ps_s[:, 1 + 2 * (c % 2), :],
                                       ACT.Copy).then_inc(proj_hi, 1)
                    for c in range(NC):
                        act.wait_ge(proj_ready, n * PROJ + NC + c + 1)
                        act.activation(vT[:, c, :], ps_s[:, 1 + 2 * (c % 2), :], ACT.Copy).then_inc(proj_hi, 1)
                    unit = 0
                    blk = 0
                    for kind, i, a in STEPS:
                        if kind == "Q":
                            j = 2 * NC + i * HPG + a
                            act.wait_ge(proj_ready, n * PROJ + j + 1)
                            if i:
                                act.wait_ge(scores_ready, n * N_UNITS + N_UNITS // 2)
                            act.activation(qT_hi[:, a, :], ps_s[:, 1 + 2 * (j % 2), :], ACT.Copy,
                                           scale=SCALE).then_inc(proj_hi, 1)
                            if i == 0 and a == 1:
                                for c in range(NC):
                                    act.wait_ge(vtr_ready, n * NC + c + 1)
                                    act.activation(v_hi[:, c * (C // P):(c + 1) * (C // P), :],
                                                   ps_t[c][:, :].rearrange("p (q d) -> p q d", q=C // P),
                                                   ACT.Copy).then_inc(v_hi_ready, 1)
                        elif kind == "S":
                            act.wait_ge(max_ready, n * N_UNITS + unit + 1)
                            if i >= 2:
                                act.wait_ge(pt_ready, n * TRI + blocks_before(i - 1))
                            keys = (i + 1) * P
                            s = 2 * (unit % 2)
                            src = ps_s[:, s:s + 2, :].rearrange("p c n -> p (c n)")[:, 0:keys]
                            act.activation(probs[:, i % 2, a, 0:keys], src, ACT.Exp,
                                           bias=negmax[:, i % 2, a:a + 1],
                                           accum_out=rowsum[:, i % 2, a:a + 1]).then_inc(exp_ready, 1)
                            unit += 1
                        elif kind == "T":
                            act.wait_ge(pt_ready, n * TRI + blk + 1)
                            if blk >= 2:
                                act.wait_ge(pv_done, n * TRI + blk - 1)
                            act.activation(pT_hi[:, blk % 2, :], ps_t[blk % 2][:, :], ACT.Copy).then_inc(pt_hi_ready, 1)
                            blk += 1
                        elif kind == "V" and a == i:
                            act.wait_ge(pv_done, n * TRI + blocks_before(i + 1))
                            act.wait_ge(dense_ready, past(n * NT + i))
                            act.activation(cT_hi[:, :], ps_ctx[:, :], ACT.Copy).then_inc(ctx_hi_ready, 1)

        @block.vector
        def _(dve):
            LINKS = 45
            dve.wait_ge(started, 4)

            def subtract(out_, whole, upper, signal):
                dve.tensor_tensor(out_, whole, upper.bitcast(F32), ALU.subtract).then_inc(signal, 1)

            for e in range(NSH):
                dve.wait_ge(ew_hi, e + 1)
                subtract(lo_slot(e), eraw[:, e, :], hi_slot(e), ew_lo)
            dve.wait_ge(consts_ready, 11)
            with dve.Fori(0, B) as b:
                base = b * LINKS
                link = [0]

                def chain(ins):
                    link[0] += 1
                    ins.then_inc(ln_chain, 1)
                    dve.wait_ge(ln_chain, base + link[0])

                def hold():
                    dve.memset(rcross[:, 0:1], 0.0)

                dve.wait_ge(x_in, b * 16 + 16)
                for t in range(NT):
                    last = dve.bn_stats(stats[:, t, :], acc[:, t, :])
                chain(last)
                hold()
                for t in range(NT):
                    last = dve.bn_aggr(mv[:, t, :], stats[:, t, :])
                chain(last)
                dve.tensor_scalar(rstd[:, :], mv[:, :, 1], EPS, None, ALU.add).then_inc(std_ready, 1)
                dve.wait_ge(std_ready, b * 2 + 2)
                chain(dve.reciprocal(rstd[:, :], std[:, :]))
                dve.wait_ge(z_out, past(b * 16))
                for t in range(NT):
                    dve.tensor_scalar(xn[:, t, :], acc[:, t, :], mv[:, t, 0:1], rstd[:, t:t + 1],
                                      ALU.subtract, ALU.mult).then_inc(xn_ready, 1)
                for t in range(NT):
                    dve.wait_ge(xhi_ready, b * NT + t + 1)
                    subtract(xT_lo[:, :, t * P:(t + 1) * P], xf[:, t % 2, :, :], xT_hi[:, :, t * P:(t + 1) * P], xlo_ready)
                dve.wait_ge(logits_ready, past(b * NT + NT))
                dve.wait_ge(consts_in, 32)
                dve.tensor_tensor(rz[:, :, :], ps_logit[:, 0:NT * E].rearrange("p (t e) -> p t e", t=NT),
                                  br_sb[:, :].unsqueeze(1).to_broadcast([P, NT, E]), ALU.add).then_inc(z_ready, 1)
                dve.wait_ge(ez_ready, b + 1)
                chain(dve.tensor_scalar(rs[:, :, :], rs[:, :, :], 1.0, None, ALU.add))
                chain(dve.reciprocal(rs[:, :, :], rs[:, :, :]))
                pairs = rs[:, :, :].rearrange("p t (g a c) -> p (t g) a c", g=G, a=2)
                chain(dve.tensor_tensor(rhi[:, :, :], pairs[:, :, :, 0], pairs[:, :, :, 1], ALU.max))
                chain(dve.tensor_tensor(rlo[:, :, :], pairs[:, :, :, 0], pairs[:, :, :, 1], ALU.min))
                chain(dve.tensor_tensor(rlo[:, :, :], rlo[:, :, :], rhi[:, :, :], ALU.add))
                chain(dve.tensor_tensor(rcross[:, :], rhi[:, :, 0], rhi[:, :, 1], ALU.add))
                chain(dve.tensor_tensor(rgw[:, :], rlo[:, :, 0], rlo[:, :, 1], ALU.max))
                chain(dve.tensor_tensor(rgw[:, :], rgw[:, :], rcross[:, :], ALU.max))
                hold()
                for t in range(NT):
                    last = dve.max(out=top_g[:, t, :], in_=rgw[:, t * G:(t + 1) * G])
                chain(last)
                chain(dve.memset(top_g[:, :, KG:8], -1.0))
                hold()
                for t in range(NT):
                    last = dve.match_replace(out=rgm[:, t * G:(t + 1) * G], in_to_replace=top_g[:, t, :],
                                             in_values=rgw[:, t * G:(t + 1) * G], imm_value=-2.0)
                chain(last)
                chain(dve.tensor_scalar(rgm[:, :], rgm[:, :], -2.0, None, ALU.is_equal))
                chain(dve.tensor_tensor(rmask[:, :, :].rearrange("p t (g c) -> p (t g) c", g=G),
                                        rs[:, :, :].rearrange("p t (g c) -> p (t g) c", g=G),
                                        rgm[:, :].unsqueeze(2).to_broadcast([P, NT * G, EG]), ALU.mult))
                hold()
                for t in range(NT):
                    last = dve.max(out=top_e[:, t, :], in_=rmask[:, t, :])
                chain(last)
                chain(dve.memset(top_e[:, :, TOPK:8], -1.0))
                hold()
                for t in range(NT):
                    last = dve.match_replace(out=rz[:, t, :], in_to_replace=top_e[:, t, :],
                                             in_values=rmask[:, t, :], imm_value=-2.0)
                chain(last)
                chain(dve.tensor_scalar(rsel[:, :, :], rz[:, :, :], -2.0, None, ALU.is_equal))
                dve.memset(rcross[:, 0:1], 0.0).then_inc(sel_ready, 1)
                sel = rsel[:, :, :].bitcast(F32)
                chain(dve.tensor_tensor(rz[:, :, :], sel, rs[:, :, :], ALU.mult))
                chain(dve.tensor_reduce(rsum[:, :], rz[:, :, :], AX.X, ALU.add))
                chain(dve.tensor_scalar(rsum[:, :], rsum[:, :], 1e-20, None, ALU.add))
                chain(dve.reciprocal(rsum[:, :], rsum[:, :]))
                chain(dve.scalar_tensor_tensor(out=gate[:, :, :], in0=rz[:, :, :], scalar=ROUTE_SCALE,
                                               in1=rsum[:, :].unsqueeze(2).to_broadcast([P, NT, E]),
                                               op0=ALU.mult, op1=ALU.mult))
                dve.wait_ge(ranks_ready, b + 1)
                ranks = ps_rank[:, 0:NT * E].rearrange("p (t e) -> p t e", t=NT)
                for t in range(NT):
                    chain(dve.tensor_tensor(seen[:, t + 1, :], seen[:, t, :],
                                            ps_rank[:, (NT + t) * E:(NT + t + 1) * E], ALU.add))
                chain(dve.tensor_tensor(rrow[:, :, :], seen[:, 0:NT, :], ranks, ALU.add))
                dve.tensor_copy(seen[:, 0, :], seen[:, NT, :]).then_inc(ranks_read, 1)
                chain(dve.tensor_tensor(rrow[:, :, :], rrow[:, :, :],
                                        row_base[:, :].unsqueeze(1).to_broadcast([P, NT, E]), ALU.add))
                chain(dve.tensor_tensor(rrow[:, :, :], rrow[:, :, :], sel, ALU.mult))
                hold()
                for t in range(NT):
                    last = dve.max(out=top_y[:, t, :], in_=rrow[:, t, :])
                chain(last)
                chain(dve.tensor_scalar(yrow_s[:, :, :], top_y[:, :, :], -1.0, None, ALU.add))
                chain(dve.tensor_scalar(bits[:, 0, :, :], yrow_s[:, :, :], P - 1, 4,
                                        ALU.bitwise_and, ALU.logical_shift_left))
                chain(dve.tensor_scalar(bits[:, 1, :, :], yrow_s[:, :, :], 7, ECAP - 1,
                                        ALU.logical_shift_right, ALU.bitwise_and))
                chain(dve.tensor_tensor(bits[:, 0, :, :], bits[:, 0, :, :], bits[:, 1, :, :], ALU.bitwise_or))
                chain(dve.tensor_scalar(bits[:, 1, :, :], yrow_s[:, :, :], E * T - T, None, ALU.bitwise_and))
                dve.wait_ge(tok_copied, past(b + 1))
                dve.tensor_tensor(tok_pos[:, :, :], bits[:, 0, :, :], bits[:, 1, :, :],
                                  ALU.bitwise_or).then_inc(tok_pos_ready, 1)
                dve.tensor_copy(y_rows[:, bass.ds(b * NT, NT), :], yrow_s[:, :, :])
                chain(dve.tensor_tensor(match[:, :, :, :],
                                        rrow[:, :, :].unsqueeze(2).to_broadcast([P, NT, TOPK, E]),
                                        top_y[:, :, 0:TOPK].unsqueeze(3).to_broadcast([P, NT, TOPK, E]), ALU.is_equal))
                chain(dve.tensor_tensor(match[:, :, :, :], match[:, :, :, :],
                                        gate[:, :, :].unsqueeze(2).to_broadcast([P, NT, TOPK, E]), ALU.mult))
                chain(dve.tensor_reduce(y_gate[:, bass.ds(b * NT, NT), :], match[:, :, :, :], AX.X, ALU.add))
                assert link[0] == LINKS, link[0]

                def add_outputs(u):
                    e, c = divmod(u, NC)
                    for q in range(CQ):
                        t = c * CQ + q
                        k = (b * UNITS + u) * CQ
                        dve.wait_ge(y_ready, past(k + q + 1))
                        dve.wait_ge(y_added, past(k + q + 1 - NT if u >= 2 else b * YA))
                        dve.tensor_tensor(acc[:, t, :], banks[q][:, :], acc[:, t, :], ALU.add).then_inc(y_added, 1)

                for u in range(UNITS):
                    dve.wait_ge(relu_ready, past((b * UNITS + u + 1) * KM))
                    dve.wait_ge(hlo_ready, past(b * UNITS + u))
                    dve.tensor_tensor(hsq[:, :, :], relu[:, u % 2, :, :], relu[:, u % 2, :, :],
                                      ALU.mult).then_inc(hsq_ready, 1)
                    dve.wait_ge(hsq_ready, past(b * UNITS + u + 1))
                    dve.wait_ge(hhi_ready, (b * UNITS + u + 1) * KM)
                    subtract(h_lo[:, u % 2, :, :], hsq[:, :, :], h_hi[:, u % 2, :, :], hlo_ready)
                    if u >= 1:
                        add_outputs(u - 1)
                add_outputs(UNITS - 1)

            last_link = [LINKS * B]

            def chain_end(ins):
                last_link[0] += 1
                ins.then_inc(ln_chain, 1)
                dve.wait_ge(ln_chain, last_link[0])

            dve.wait_ge(y_added, past(B * YA))
            chain_end(dve.tensor_scalar(pairs_f[:, :], seen[:, 0, :], float(PR - 1), None, ALU.add))
            chain_end(dve.tensor_copy(pairs_i[:, :], pairs_f[:, :]))
            chain_end(dve.tensor_scalar(pairs_i[:, :], pairs_i[:, :], 8, None, ALU.logical_shift_right))
            chain_end(dve.tensor_copy(pairs_f[:, :], pairs_i[:, :]))
            chain_end(dve.tensor_scalar(pairs_f[:, :], pairs_f[:, :], 1.0, None, ALU.max))
            chain_end(dve.tensor_tensor_scan(scan_f[:, :], scan_ones[:, :], pairs_f[:, :], 0.0, ALU.mult, ALU.add))
            chain_end(dve.memset(first_pair[:, :, 0:1], 0))
            for row in range(2):
                chain_end(dve.tensor_copy(first_pair[:, row, 1:E + 1], scan_f[:, :]))
            dve.tensor_scalar(first_pair[:, 1, E:E + 1], scan_f[:, E - 1:E], 1.0, None, ALU.add).then_inc(pairs_ready, 1)
            dve.wait_ge(pairs_ready, 1)
            chain_end(dve.tensor_tensor(scan_f[:, :], scan_f[:, :], pairs_f[:, :], ALU.subtract))
            chain_end(dve.tensor_scalar(scan_f[:, :], scan_f[:, :], float(PR), None, ALU.mult))
            chain_end(dve.tensor_scalar(row_base[:, :], row_base[:, :], -1.0, None, ALU.add))
            chain_end(dve.tensor_tensor(scan_f[:, :], scan_f[:, :], row_base[:, :], ALU.subtract))
            for b in range(B):
                rows = y_rows[:, b * NT:(b + 1) * NT, :]
                chain_end(dve.tensor_copy(top_y[:, :, :], rows))
                chain_end(dve.tensor_scalar(yrow_s[:, :, :], rows, E * T - T, None, ALU.bitwise_and))
                chain_end(dve.tensor_copy(top_e[:, :, :], yrow_s[:, :, :]))
                chain_end(dve.tensor_tensor(match[:, :, :, :],
                                            top_e[:, :, 0:TOPK].unsqueeze(3).to_broadcast([P, NT, TOPK, E]),
                                            row_base[:, :].unsqueeze(1).unsqueeze(1).to_broadcast([P, NT, TOPK, E]),
                                            ALU.is_equal))
                chain_end(dve.tensor_tensor(match[:, :, :, :], match[:, :, :, :],
                                            scan_f[:, :].unsqueeze(1).unsqueeze(1).to_broadcast([P, NT, TOPK, E]),
                                            ALU.mult))
                chain_end(dve.tensor_reduce(top_e[:, :, 0:TOPK], match[:, :, :, :], AX.X, ALU.add))
                chain_end(dve.tensor_tensor(rows[:, :, 0:TOPK], top_y[:, :, 0:TOPK], top_e[:, :, 0:TOPK], ALU.add))
            dve.memset(rcross[:, 0:1], 0.0).then_inc(y_rows_ready, 1)
            dve.wait_ge(xn_out, 16 * B)

            def lower_tokens(q):
                for r in range(ROWS):
                    dve.wait_ge(mx_hi, q * ROWS + (r + 1))
                    rr = slice(r * P, (r + 1) * P)
                    subtract(xgT_lo[:, :, rr], ps_x[r].rearrange("p (k n) -> p k n", k=KD), xgT_hi[:, :, rr], mx_lo)

            def copy_output(q):
                dve.wait_ge(my_ready, past(q * ROWS))
                dve.wait_ge(y_stored, past((q - 2) * 16, Y_START))
                dve.tensor_copy(ysb[:, bass.ds((q + 1) % 2, 1), 0, :].rearrange("p s d -> p (s d)"),
                                ps_y[0][:, :]).then_inc(y0_copied, 1)

            for e in range(2):
                dve.wait_ge(ew_hi, NSH + e + 1)
                subtract(lo_slot(e), eraw[:, e, :], hi_slot(e), ew_lo)
            lower_tokens(0)

            def expert_lowers(e, s, lo, hi, es):
                dve.wait_ge(ew_hi, e + (NSH + 3))
                subtract(lo_slot((s + 2) % SLOTS), eraw[:, s % 2, :], hi_slot((s + 2) % SLOTS), ew_lo)
                with dve.Fori(lo, hi) as p:
                    copy_output(p)
                    for m in range(KM):
                        dve.wait_ge(mrelu_ready, past(p * KM + m + 1))
                        dve.wait_ge(mhlo_ready, past(p * KM))
                        dve.tensor_tensor(mhsq[:, m, :], mrelu[:, m, :], mrelu[:, m, :], ALU.mult).then_inc(mhsq_ready, 1)
                        dve.wait_ge(mhsq_ready, past(p * KM + m + 1))
                        dve.wait_ge(mhhi_ready, p * KM + m + 1)
                        subtract(mh_lo[:, m, :], mhsq[:, m, :], mh_hi[:, m, :], mhlo_ready)
                    lower_tokens(p + 1)

            over_experts(dve, expert_lowers)
            copy_output(pair_bound(dve, E))
            with dve.Fori(0, B) as b:
                for t in range(NT):
                    dve.wait_ge(xr_hi, past(b * NT + t + 1))
                    ts = slice(t * P, (t + 1) * P)
                    subtract(xT_lo[:, :, ts], ps_t[t % 2][:, :].rearrange("p (k n) -> p k n", k=KD), xT_hi[:, :, ts], xr_lo)
                with dve.Fori(0, GROUPS) as g:
                    n = b * GROUPS + g
                    for c in range(PIECES):
                        dve.wait_ge(aw_hi, past(n * PIECES + c + 1))
                        dve.tensor_tensor(wa_lo[:, c * PIECE:(c + 1) * PIECE], araw[:, c % 2, :],
                                          wa_hi[:, c * PIECE:(c + 1) * PIECE].bitcast(F32),
                                          ALU.subtract).then_inc(aw_lo, 1)
                    for c in range(NC):
                        dve.wait_ge(proj_hi, n * PROJ + c + 1)
                        dve.tensor_tensor(kT_lo[:, c * C:(c + 1) * C], ps_s[:, 1 + 2 * (c % 2), :],
                                          kT_hi[:, c * C:(c + 1) * C].bitcast(F32), ALU.subtract).then_inc(proj_lo, 1)
                    unit = 0
                    blk = 0

                    def norm(u, i, h, wait_=True):
                        dve.wait_ge(exp_ready, past(n * N_UNITS + u + 1))
                        dve.reciprocal(rnorm[:, i % 2, h:h + 1], rowsum[:, i % 2, h:h + 1]).then_inc(rnorm_ready, 1)
                        dve.wait_ge(rnorm_ready, n * N_UNITS + u + 1)
                        pr = probs[:, i % 2, h, 0:(i + 1) * P]
                        dve.tensor_scalar(pr, pr, rnorm[:, i % 2, h:h + 1], None, ALU.mult).then_inc(probs_ready, 1)

                    combined = 0
                    pending = None
                    for kind, i, a in STEPS:
                        if kind == "Q":
                            j = 2 * NC + i * HPG + a
                            dve.wait_ge(proj_hi, n * PROJ + j + 1)
                            dve.scalar_tensor_tensor(out=qT_lo[:, a, :], in0=ps_s[:, 1 + 2 * (j % 2), :],
                                                     scalar=SCALE, in1=qT_hi[:, a, :].bitcast(F32),
                                                     op0=ALU.mult, op1=ALU.subtract).then_inc(proj_lo, 1)
                            if i == 0 and a == 1:
                                for c in range(NC):
                                    dve.wait_ge(v_hi_ready, n * NC + c + 1)
                                    vs = slice(c * (C // P), (c + 1) * (C // P))
                                    dve.tensor_tensor(v_lo[:, vs, :],
                                                      ps_t[c][:, :].rearrange("p (q d) -> p q d", q=C // P),
                                                      v_hi[:, vs, :].bitcast(F32), ALU.subtract).then_inc(v_lo_ready, 1)
                        elif kind == "S":
                            dve.wait_ge(scores_ready, n * N_UNITS + unit + 1)
                            keys = (i + 1) * P
                            s = 2 * (unit % 2)
                            src = ps_s[:, s:s + 2, :].rearrange("p c n -> p (c n)")[:, 0:keys]
                            dve.tensor_reduce(negmax[:, i % 2, a:a + 1], src, AX.X, ALU.max,
                                              negate=True).then_inc(max_ready, 1)
                            if pending:
                                norm(*pending)
                            pending = (unit, i, a)
                            unit += 1
                        elif kind == "T":
                            if pending and pending[1] == i:
                                norm(*pending)
                                pending = None
                            dve.wait_ge(pt_hi_ready, n * TRI + blk + 1)
                            dve.tensor_tensor(pT_lo[:, blk % 2, :], ps_t[blk % 2][:, :],
                                              pT_hi[:, blk % 2, :].bitcast(F32), ALU.subtract).then_inc(pt_lo_ready, 1)
                            blk += 1
                        elif kind == "V" and a == i:
                            dve.wait_ge(ctx_hi_ready, n * NT + i + 1)
                            dve.tensor_tensor(cT_lo[:, :], ps_ctx[:, :], cT_hi[:, :].bitcast(F32),
                                              ALU.subtract).then_inc(ctx_lo_ready, 1)
                            if i >= 2:
                                dve.wait_ge(dense_added, past(n * NT + i))
                                for j in range(combined, combined + 2):
                                    tile = j // TOPK
                                    at = g * (NT // GROUPS) + tile
                                    dve.wait_ge(comb_in[j % COMB], (n * (NCOMB // COMB) + j // COMB + 1) * 16)
                                    dve.wait_ge(comb_added, past(n * NCOMB + j))
                                    acc_t = acc[:, bass.ds(at, 1), :].rearrange("p t d -> p (t d)")
                                    w_t = y_gate[:, bass.ds(b * NT + at, 1), j % TOPK]
                                    dve.scalar_tensor_tensor(out=acc_t, in0=comb[:, j % COMB, :], scalar=w_t, in1=acc_t,
                                                             op0=ALU.mult, op1=ALU.add).then_inc(comb_added, 1)
                                combined += 2
                        elif kind == "D":
                            if pending and pending[1] == i + 1:
                                norm(*pending)
                                pending = None
                            dve.wait_ge(dense_ready, past(n * NT + i + 1))
                            if i == 0:
                                dve.wait_ge(dense_added, past(n * NT))
                                dve.wait_ge(z_in, (b + 1) * 16)
                            dve.wait_ge(comb_added, past(n * NCOMB + combined))
                            dve.tensor_tensor(acc[:, i, :], acc[:, i, :], ps_d[:, :], ALU.add).then_inc(dense_added, 1)


def kernel(L0_attn_x, L0_attn_w_q, L0_attn_w_kv, L0_attn_w_dense, L0_ffn_Wr, L0_ffn_br, L0_ffn_W1, L0_ffn_W2,
           L0_ffn_Ws1, L0_ffn_Ws2):
    import concourse.bacc as bacc
    from concourse.bass_utils import run_bass_kernel_spmd

    wq = np.asarray(L0_attn_w_q).reshape(KD, P, GROUPS, HPG * HD).transpose(2, 1, 0, 3).reshape(GROUPS, P, WQ_COLS)
    wkv = np.asarray(L0_attn_w_kv).reshape(KD, P, 2, GROUPS, HD).transpose(3, 1, 0, 2, 4).reshape(GROUPS, P, WKV_COLS)
    wd = np.asarray(L0_attn_w_dense).reshape(GROUPS, HPG, P, D).transpose(0, 2, 1, 3).reshape(GROUPS, P, WD_COLS)
    wa = np.ascontiguousarray(np.concatenate([wq, wkv, wd], axis=2).reshape(GROUPS * P, WA_COLS))
    w1 = np.concatenate([np.asarray(L0_ffn_W1), np.asarray(L0_ffn_Ws1).reshape(NSH, M, D)], axis=0)
    w1 = w1.reshape(E + NSH, M, KD, P).transpose(0, 3, 2, 1).reshape(E + NSH, P, KD * M)
    w2 = np.concatenate([np.asarray(L0_ffn_W2), np.asarray(L0_ffn_Ws2).reshape(D, NSH, M).transpose(1, 0, 2)], axis=0)
    w2 = w2.reshape(E + NSH, D, KM, P).transpose(0, 3, 2, 1).reshape(E + NSH, P, KM * D)
    we = np.concatenate([w1, w2], axis=2)
    we = np.ascontiguousarray(np.concatenate([we, we[:AHEAD - NSH]], axis=0).reshape((E + AHEAD) * P, W_COLS))
    wr = np.ascontiguousarray(np.asarray(L0_ffn_Wr).reshape(E, KD, P).transpose(2, 1, 0))
    br = np.ascontiguousarray(np.broadcast_to(np.asarray(L0_ffn_br), (P, E)))
    x = np.ascontiguousarray(L0_attn_x)

    nc = bacc.Bacc("TRN2", target_bir_lowering=False, num_devices=1)
    arrays = {"x": x, "wa": wa, "we": we, "wr": wr, "br": br}
    aps = [nc.dram_tensor(k, a.shape, mybir.dt.from_np(a.dtype), kind="ExternalInput").ap() for k, a in arrays.items()]
    out = nc.dram_tensor("out", (B, SQ, D), F32, kind="ExternalOutput").ap()
    moe_attention_kernel(nc, *aps, out)
    r = run_bass_kernel_spmd(nc, [arrays], core_ids=[0])
    return r.results[0]["out"]
```

```python
import numpy as np

import concourse.bass as bass
from concourse import mybir
from contextlib import ExitStack

F32 = mybir.dt.float32
F32R = mybir.dt.float32r
I32 = mybir.dt.int32
ALU = mybir.AluOpType
ACT = mybir.ActivationFunctionType
AX = mybir.AxisListType

P = 128
B, SQ, D = 2, 1024, 512
KD = D // P
NT = SQ // P
HEADS, GROUPS, HD = 16, 4, 128
HPG = HEADS // GROUPS
SCALE = float(HD) ** -0.5
E, M = 32, 256
SH = 512
NSH = SH // M
KM = M // P
G, EG, KG, TOPK = 8, 4, 4, 6
ROUTE_SCALE = 2.5
EPS = 1e-5
MASKED = -3.0e38

W_COLS = KD * M + KM * D
WQ_COLS, WKV_COLS, WD_COLS = KD * HPG * HD, KD * 2 * HD, HPG * D
PIECE = 1024
WA_COLS = WQ_COLS + WKV_COLS + WD_COLS
PIECES = WA_COLS // PIECE
C = 512
NC = SQ // C
UNITS = NSH * NC
T = B * SQ
TILES = B * NT
ROWS = 2
PR = ROWS * P
ECAP = T // P
AHEAD = 3
SLOTS = 4
COMB = 3
PAIRS = T * TOPK // PR + E
NCOMB = TOPK * NT // GROUPS
Y_START = 1 + 3 * 16
X_START = 3
TRI = NT * (NT + 1) // 2
RING = 3


def past(n, start=1):
    return n + start


GROUP_ORDER = (
    "S10 E10 S11 N10 T00 C0 E11 W3 Q10 S12 W4 E12 S13 N11 E13 N12 N13 Q11 S20 V00 E20 S21 E21 N20 F0 Q12 T10 S22 "
    "S23 E22 D0 E23 C1 N21 T11 N22 S30 S31 E30 N23 C2 Q13 N30 V10 E31 V11 F1 T20 S32 N31 T21 E32 S33 N32 T22 E33 "
    "V20 D1 N33 S40 S41 E40 V21 N40 T30 E41 C3 V22 F2 S42 T31 E42 S43 N41 V30 N42 W0+ T32 E43 N43 D2 S50 T33 V31 "
    "S51 E50 T40 V32 N50 V33 F3 E51 S52 T41 T42 E52 S53 E53 N51 V40 T43 N52 V41 N53 T44 S60 S61 V42 D3 E60 T50 "
    "N60 V43 E61 T51 V44 F4 S62 S63 E62 T52 V50 E63 N61 V51 T53 S70 N62 T54 S71 V52 T55 N63 V53 C4 V54 W1+ D4 "
    "E70 C5 T60 V55 F5 T61 S72 N70 E71 T62 E72 C6 V60 V61 S73 W2+ N71 N72 T63 E73 T64 C7 D5 K0+ V62 K1+ V63 P0+ "
    "V64 N73 T65 C8 T66 P1+ T70 V65 V66 T71 F6 Q00+ Q01+ C9 Q02+ T72 Q03+ V70 T73 V71 T74 S00+ V72 T75 V73 V74 "
    "T76 C10 E00+ T77 C11 V75 D6 N00+ V76 V77 S01+ F7 S02+ E01+ X+ S03+ E02+ N01+ E03+ N02+ N03+ D7"
)
FIRST_ORDER = ("W0 W1 W2 K0 K1 P0 P1 Q00 Q01 Q02 Q03 S00 E00 S01 E01 N00 X S02 E02 N01 S03 E03 N02 N03")


def steps_of(order):
    steps = []
    for word in order.split():
        name = word.rstrip("+")
        kind, digits = name[0], name[1:]
        if kind in "QSENTV":
            i, a = int(digits[0]), int(digits[1])
        elif kind in "WKP":
            i, a = 0, int(digits)
        else:
            i, a = int(digits or 0), 0
        steps.append((kind, i, a, int(word.endswith("+"))))
    return steps


FIRST, GROUP = steps_of(FIRST_ORDER), steps_of(GROUP_ORDER)
LAST = [step for step in GROUP if not step[3]]


def blocks_before(i):
    return i * (i + 1) // 2


def moe_attention_kernel(nc, x, wa, we, wr, br, out):
    xb = x.rearrange("b (t p) d -> p (b t) d", p=P)
    outb = out.rearrange("b (t p) d -> p (b t) d", p=P)

    xn_d = nc.dram_tensor("normed_tokens", (T, D), F32, kind="Internal").ap()
    z_d = nc.dram_tensor("residual_and_shared", (SQ, D), F32, kind="Internal").ap()
    y_d = nc.dram_tensor("expert_outputs", ((PAIRS + 1) * PR, D), F32, kind="Internal").ap()
    tok_d = nc.dram_tensor("expert_tokens", (E * T, 1), I32, kind="Internal").ap()
    xn_b = xn_d.rearrange("(t p) d -> p t d", p=P)
    tok_rows = tok_d.rearrange("(p n) o -> p (n o)", p=P)
    tok_b = tok_d.rearrange("(e p c) o -> p e (c o)", p=P, c=ECAP)

    with ExitStack() as ctx:
        def sb(name, shape, dt, stack=ctx):
            return stack.enter_context(nc.sbuf_tensor(name, shape, dt))

        def sem(name):
            return ctx.enter_context(nc.semaphore(name))

        acc = sb("acc", [P, NT, D], F32)
        xT_hi = sb("xT_hi", [P, KD, SQ], F32R)
        xT_lo = sb("xT_lo", [P, KD, SQ], F32R)
        ident = sb("ident", [P, P], F32)
        ident_r = sb("ident_r", [P, P], F32R)
        causal = sb("causal", [P, P], F32)
        causal_r = sb("causal_r", [P, P], F32R)
        y_rows = sb("y_rows", [P, TILES, 8], I32)
        y_gate = sb("y_gate", [P, TILES, TOPK], F32)
        tok_idx = sb("tok_idx", [P, E * ECAP + ROWS], I32)
        first_pair = sb("first_pair", [P, 2, E + 1], I32)
        comb_idx = sb("comb_idx", [P, NCOMB], I32)
        comb = sb("comb", [P, COMB, D], F32)
        araw = sb("araw", [P, 2, PIECE], F32)
        settled = sb("settled", [P, NCOMB], F32)

        with ExitStack() as room:
            eraw = sb("eraw", [P, 2, W_COLS], F32, room)
            w_hi01 = sb("w_hi01", [P, 2, W_COLS], F32R, room)
            w_lo01 = sb("w_lo01", [P, 2, W_COLS], F32R, room)
            with ExitStack() as inner:
                xn = sb("xn", [P, NT, D], F32, inner)
                xf = sb("xf", [P, 2, KD, P], F32, inner)
                relu = sb("relu", [P, 2, KM, C], F32, inner)
                hsq = sb("hsq", [P, KM, C], F32, inner)
                h_hi = sb("h_hi", [P, 2, KM, C], F32R, inner)
                h_lo = sb("h_lo", [P, 2, KM, C], F32R, inner)
                wr_sb = sb("wr_sb", [P, KD, E], F32, inner)
                br_sb = sb("br_sb", [P, E], F32, inner)
                zeros = sb("zeros", [P, T * E // P], I32, inner)
                tok_all = sb("tok_all", [P, TILES], I32, inner)
                tok_s = sb("tok_s", [P, NT], I32, inner)
                before = sb("before", [P, P], F32R, inner)
                ones = sb("ones", [P, P], F32R, inner)
                tri = sb("tri", [P, P], F32, inner)
                row_base = sb("row_base", [P, E], F32, inner)
                stats = sb("stats", [P, NT, 6], F32, inner)
                mv = sb("mv", [P, NT, 2], F32, inner)
                std = sb("std", [P, NT], F32, inner)
                rstd = sb("rstd", [P, NT], F32, inner)
                rz = sb("rz", [P, NT, E], F32, inner)
                rs = sb("rs", [P, NT, E], F32, inner)
                rhi = sb("rhi", [P, NT * G, 2], F32, inner)
                rlo = sb("rlo", [P, NT * G, 2], F32, inner)
                rcross = sb("rcross", [P, NT * G], F32, inner)
                rgw = sb("rgw", [P, NT * G], F32, inner)
                top_g = sb("top_g", [P, NT, 8], F32, inner)
                rgm = sb("rgm", [P, NT * G], F32, inner)
                rmask = sb("rmask", [P, NT, E], F32, inner)
                top_e = sb("top_e", [P, NT, 8], F32, inner)
                rsel = sb("rsel", [P, NT, E], F32R, inner)
                gate = sb("gate", [P, NT, E], F32, inner)
                rsum = sb("rsum", [P, NT], F32, inner)
                seen = sb("seen", [P, NT + 1, E], F32, inner)
                rrow = sb("rrow", [P, NT, E], F32, inner)
                top_y = sb("top_y", [P, NT, 8], F32, inner)
                match = sb("match", [P, NT, TOPK, E], F32, inner)
                yrow_s = sb("yrow_s", [P, NT, 8], I32, inner)
                bits = sb("bits", [P, 2, NT, 8], I32, inner)
                tok_pos = sb("tok_pos", [P, NT, 8], I32, inner)
                pairs_i = sb("pairs_i", [P, E], I32, inner)
                pairs_f = sb("pairs_f", [P, E], F32, inner)
                scan_ones = sb("scan_ones", [P, E], F32, inner)
                scan_f = sb("scan_f", [P, E], F32, inner)
            with ExitStack() as inner:
                w_hi23 = sb("w_hi23", [P, 2, W_COLS], F32R, inner)
                w_lo23 = sb("w_lo23", [P, 2, W_COLS], F32R, inner)
                pair_idx = sb("pair_idx", [P, 2, ROWS], I32, inner)
                xg = sb("xg", [P, 2, ROWS, D], F32, inner)
                xgT_hi = sb("xgT_hi", [P, KD, PR], F32R, inner)
                xgT_lo = sb("xgT_lo", [P, KD, PR], F32R, inner)
                mrelu = sb("mrelu", [P, KM, PR], F32, inner)
                mhsq = sb("mhsq", [P, KM, PR], F32, inner)
                mh_hi = sb("mh_hi", [P, KM, PR], F32R, inner)
                mh_lo = sb("mh_lo", [P, KM, PR], F32R, inner)
                ysb = sb("ysb", [P, 2, ROWS, D], F32, inner)
        with ExitStack() as room:
            wa_hi = sb("wa_hi", [P, WA_COLS], F32R, room)
            wa_lo = sb("wa_lo", [P, WA_COLS], F32R, room)
            qT_hi = sb("qT_hi", [P, NC, HPG, C], F32R, room)
            qT_lo = sb("qT_lo", [P, NC, HPG, C], F32R, room)
            kT_hi = sb("kT_hi", [P, SQ], F32R, room)
            kT_lo = sb("kT_lo", [P, SQ], F32R, room)
            vT = sb("vT", [P, NC, C], F32, room)
            v_hi = sb("v_hi", [P, NT, HD], F32R, room)
            v_lo = sb("v_lo", [P, NT, HD], F32R, room)
            probs = sb("probs", [P, 2, HPG, SQ], F32, room)
            pT_hi = sb("pT_hi", [P, RING, HPG * P], F32R, room)
            pT_lo = sb("pT_lo", [P, RING, HPG * P], F32R, room)
            cT_hi = sb("cT_hi", [P, HPG * P], F32R, room)
            cT_lo = sb("cT_lo", [P, HPG * P], F32R, room)
            negmax = sb("negmax", [P, 2, HPG], F32, room)
            rowsum = sb("rowsum", [P, 2, HPG], F32, room)
            rnorm = sb("rnorm", [P, 2, HPG], F32, room)
        xn_again = [w[:, 0:SQ * D // P // 2].bitcast(F32).rearrange("p (t d) -> p t d", d=D) for w in (wa_hi, wa_lo)]

        banks = [ctx.enter_context(nc.psum_tensor(f"bank{i}", [P, 512], F32)) for i in range(4, 8)]
        ps_s = ctx.enter_context(nc.psum_tensor("ps_s", [P, 4, 512], F32))
        ps_t = banks[0:2]
        ps_ctx = banks[2]
        ps_d = banks[3]
        ps_logit = banks[2]
        ps_rank = banks[3]
        ps_x = [ps_s[:, 2, :], ps_s[:, 3, :]]
        ps_y = banks[0:2]

        consts_in = sem("consts_in")
        x_in = sem("x_in")
        acc_in = sem("acc_in")
        z_out = sem("z_out")
        z_in = sem("z_in")
        xn_out = sem("xn_out")
        xn_in = sem("xn_in")
        out_done = sem("out_done")
        pool_chain = sem("pool_chain")
        consts_ready = sem("consts_ready")
        tok_zeroed = sem("tok_zeroed")
        ln_chain = sem("ln_chain")
        std_ready = sem("std_ready")
        xn_ready = sem("xn_ready")
        xnT_ready = sem("xnT_ready")
        xf_ready = sem("xf_ready")
        xhi_ready = sem("xhi_ready")
        xlo_ready = sem("xlo_ready")
        logits_ready = sem("logits_ready")
        z_ready = sem("z_ready")
        ez_ready = sem("ez_ready")
        sel_ready = sem("sel_ready")
        ranks_ready = sem("ranks_ready")
        ranks_read = sem("ranks_read")
        tok_pos_ready = sem("tok_pos_ready")
        tok_copied = sem("tok_copied")
        tok_out = sem("tok_out")
        tok_in = sem("tok_in")
        pairs_ready = sem("pairs_ready")
        y_rows_ready = sem("y_rows_ready")
        eraw_in = [sem("eraw_in0"), sem("eraw_in1")]
        ew_hi = sem("ew_hi")
        ew_lo = sem("ew_lo")
        h_ready = sem("h_ready")
        relu_ready = sem("relu_ready")
        hhi_ready = sem("hhi_ready")
        hsq_ready = sem("hsq_ready")
        hlo_ready = sem("hlo_ready")
        y_ready = sem("y_ready")
        y_added = sem("y_added")
        idx_ready = sem("idx_ready")
        xg_in = [sem("xg_in0"), sem("xg_in1")]
        mx_ready = sem("mx_ready")
        mx_hi = sem("mx_hi")
        mx_lo = sem("mx_lo")
        mh_ready = sem("mh_ready")
        mrelu_ready = sem("mrelu_ready")
        mhsq_ready = sem("mhsq_ready")
        mhhi_ready = sem("mhhi_ready")
        mhlo_ready = sem("mhlo_ready")
        my_ready = sem("my_ready")
        y0_copied = sem("y0_copied")
        y1_copied = sem("y1_copied")
        y_stored = sem("y_stored")
        room_free = sem("room_free")
        xr_ready = sem("xr_ready")
        xr_hi = sem("xr_hi")
        xr_lo = sem("xr_lo")
        comb_idx_ready = sem("comb_idx_ready")
        comb_in = [sem(f"comb_in{i}") for i in range(COMB)]
        comb_added = sem("comb_added")
        araw_in = [sem("araw_in0"), sem("araw_in1")]
        aw_hi = sem("aw_hi")
        aw_lo = sem("aw_lo")
        proj_ready = sem("proj_ready")
        proj_hi = sem("proj_hi")
        proj_lo = sem("proj_lo")
        vtr_ready = sem("vtr_ready")
        v_hi_ready = sem("v_hi_ready")
        v_lo_ready = sem("v_lo_ready")
        scores_ready = sem("scores_ready")
        max_ready = sem("max_ready")
        exp_ready = sem("exp_ready")
        rnorm_ready = sem("rnorm_ready")
        probs_ready = sem("probs_ready")
        pt_ready = sem("pt_ready")
        pt_hi_ready = sem("pt_hi_ready")
        pt_lo_ready = sem("pt_lo_ready")
        pv_done = sem("pv_done")
        ctx_hi_ready = sem("ctx_hi_ready")
        ctx_lo_ready = sem("ctx_lo_ready")
        dense_ready = sem("dense_ready")
        dense_added = sem("dense_added")
        start_at_one = (ranks_read, out_done, xf_ready, logits_ready, xlo_ready, relu_ready, hsq_ready, hlo_ready,
                        y_ready, y_added, tok_copied, mrelu_ready, mhsq_ready, mhlo_ready, my_ready,
                        y0_copied, y1_copied, z_in, comb_added, aw_hi, aw_lo, exp_ready, ctx_lo_ready,
                        dense_ready, dense_added)
        started = sem("started")

        PROJ = 2 * NC + 2 * HPG
        SPLIT = PROJ - NC
        N_UNITS = NT * HPG
        CQ = C // P
        YA = UNITS * CQ
        SCATTERS = TOPK * NT
        ALL_IN = [16 * ((E + AHEAD + NSH + 1) // 2), 16 * ((E + AHEAD + NSH) // 2)]

        wq = lambda w: w[:, 0:WQ_COLS].rearrange("p (k n) -> p k n", k=KD)
        wkv = lambda w: w[:, WQ_COLS:WQ_COLS + WKV_COLS].rearrange("p (k n) -> p k n", k=KD)
        wd = lambda w: w[:, WQ_COLS + WKV_COLS:WA_COLS].rearrange("p (h n) -> p h n", h=HPG)
        w1 = lambda w: w[:, 0:KD * M].rearrange("p (k m) -> p k m", k=KD)
        w2 = lambda w: w[:, KD * M:W_COLS].rearrange("p (k n) -> p k n", k=KM)
        hi_slot = lambda s: (w_hi01, w_hi23)[s // 2][:, s % 2, :]
        lo_slot = lambda s: (w_lo01, w_lo23)[s // 2][:, s % 2, :]

        def pair_bound(eng, e, row=0):
            return eng.value_load(first_pair[0:1, row, bass.ds(e, 1)], min_val=0, max_val=PAIRS + row)

        def over_experts(eng, body, row=0):
            with eng.Fori(0, E // SLOTS) as es:
                lo = pair_bound(eng, es * SLOTS, row)
                for s in range(SLOTS):
                    hi = pair_bound(eng, es * SLOTS + s + 1, row)
                    body(es * SLOTS + s, s, lo, hi, es)
                    lo = hi

        def attend_groups(eng, attend, turn):
            attend(FIRST, turn * GROUPS)
            with eng.Fori(0, GROUPS - 1) as g:
                attend(GROUP, turn * GROUPS + g, g)
            attend(LAST, turn * GROUPS + (GROUPS - 1), GROUPS - 1)

        def settle(pool, c=0):
            pool.tensor_tensor(settled[:, c:c + 1], ident[:, 0:1], ident[:, 0:1], ALU.mult)

        block = ctx.enter_context(nc.Block())

        @block.sync
        def _(sp):
            sp.wait_ge(started, 4)
            x_tiles = lambda b: xb[:, b * NT:(b + 1) * NT, :]
            xn_tiles = lambda b: xn_b[:, b * NT:(b + 1) * NT, :]
            sp.dma_start(xn[:, :, :], x_tiles(0)).then_inc(x_in, 16)
            for e in range(NSH):
                sp.dma_start(eraw[:, e, :], we[(E + e) * P:(E + e + 1) * P, :]).then_inc(eraw_in[e], 16)
            sp.dma_start(wr_sb[:, :, :], wr).then_inc(consts_in, 16)
            sp.dma_start(br_sb[:, :], br).then_inc(consts_in, 16)
            sp.dma_start(acc[:, :, :], x_tiles(1)).then_inc(acc_in, 16)
            sp.wait_ge(consts_ready, 4)
            sp.dma_start(tok_rows, zeros[:, :]).then_inc(tok_zeroed, 16)
            for b in range(B):
                sp.wait_ge(xn_ready, (b + 1) * NT)
                sp.dma_start(xn_tiles(b), xn[:, :, :]).then_inc(xn_out, 16)
                sp.wait_ge(xn_out, (b + 1) * 16)
                sp.wait_ge(xnT_ready, (b + 1) * NT)
                sp.dma_start(xn[:, :, :], x_tiles(1) if b == 0 else xn_tiles(0)).then_inc(x_in, 16)
            sp.wait_ge(y_added, past(YA))
            sp.dma_start(z_d.rearrange("(t p) d -> p t d", p=P), acc[:, :, :]).then_inc(z_out, 16)
            sp.wait_ge(z_out, 16)
            sp.dma_start(acc[:, :, :], x_tiles(0)).then_inc(acc_in, 16)
            sp.wait_ge(pairs_ready, 1)
            for e in range(AHEAD):
                sp.wait_ge(ew_lo, NSH + max(e - 1, 0))
                sp.dma_start(eraw[:, e % 2, :], we[e * P:(e + 1) * P, :]).then_inc(eraw_in[e % 2], 16)
                if e == 1:
                    sp.wait_ge(tok_out, B * SCATTERS * 16)
                    sp.dma_start(tok_idx[:, 0:E * ECAP].rearrange("p (e c) -> p e c", e=E), tok_b).then_inc(tok_in, 16)

            def load_piece(n, g, c):
                if c or not isinstance(n, int):
                    sp.wait_ge(aw_hi, past(n * PIECES + max(c - 1, 0)))
                    sp.wait_ge(aw_lo, past(n * PIECES + max(c - 1, 0)))
                sp.dma_start(araw[:, c % 2, :], wa[bass.ds(g * P, P), c * PIECE:(c + 1) * PIECE]).then_inc(araw_in[c % 2], 16)

            load_piece(0, 0, 0)
            load_piece(0, 0, 1)

            def store_pairs(e, s, lo, hi, es):
                sp.wait_ge(ew_lo, e + (NSH + 2))
                sp.dma_start(eraw[:, (s + AHEAD) % 2, :],
                             we[bass.ds((e + AHEAD) * P, P), :]).then_inc(eraw_in[(s + AHEAD) % 2], 16)
                with sp.Fori(lo, hi) as p:
                    sp.wait_ge(y0_copied, past(p + 2))
                    sp.wait_ge(y1_copied, past(p + 2))
                    sp.wait_ge(y_stored, past(p * 16, Y_START))
                    sp.dma_start(y_d[bass.ds(p * PR, PR), :].rearrange("(r p) d -> p r d", p=P),
                                 ysb[:, bass.ds(p % 2, 1), :, :].rearrange("p s r d -> p (s r) d")).then_inc(y_stored, 16)

            over_experts(sp, store_pairs)
            last = pair_bound(sp, E)
            sp.wait_ge(ew_lo, NSH + E + 2)
            sp.wait_ge(mx_lo, (last + 1) * ROWS)
            sp.sem_inc(room_free, 1)
            sp.wait_ge(y_stored, past(last * 16, Y_START))
            for s in range(2):
                sp.wait_ge(eraw_in[s], ALL_IN[s])
            sp.sem_inc(room_free, 1)
            load_piece(0, 0, 2)
            with sp.Fori(last, PAIRS + 1) as p:
                sp.dma_start(y_d[bass.ds(p * PR, PR), :].rearrange("(r p) d -> p r d", p=P),
                             xT_hi[:, 0, :].bitcast(F32).rearrange("p (r d) -> p r d", r=ROWS)).then_inc(y_stored, 16)
            with sp.Fori(0, B) as turn:
                with sp.Fori(0, GROUPS - 1) as g:
                    n = turn * GROUPS + g
                    load_piece(n, g, 3)
                    load_piece(n, g, 4)
                    for c in range(3):
                        load_piece(n + 1, g + 1, c)
                n = turn * GROUPS + (GROUPS - 1)
                load_piece(n, GROUPS - 1, 3)
                load_piece(n, GROUPS - 1, 4)
                with sp.If(turn == 0):
                    sp.wait_ge(proj_ready, GROUPS * PROJ)
                    for half in range(2):
                        sp.dma_start(xn_again[half], xn_b[:, NT + half * (NT // 2):NT + (half + 1) * (NT // 2), :]).then_inc(xn_in, 16)
                    load_piece(n + 1, 0, 0)
                    load_piece(n + 1, 0, 1)
                sp.wait_ge(dense_added, past((turn + 1) * (GROUPS * NT)))
                sp.wait_ge(comb_added, past((turn + 1) * (GROUPS * NCOMB)))
                sp.dma_start(outb[:, bass.ds(turn * NT, NT), :], acc[:, :, :]).then_inc(out_done, 16)
                with sp.If(turn == 0):
                    sp.wait_ge(out_done, past(16))
                    sp.dma_start(acc[:, :, :], z_d.rearrange("(t p) d -> p t d", p=P)).then_inc(z_in, 16)
                    load_piece(n + 1, 0, 2)
            sp.wait_ge(out_done, past(16 * B))
            sp.wait_ge(xn_out, 16 * B)
            sp.wait_ge(tok_zeroed, 16)

        @block.gpsimd
        def _(pool):
            for s in start_at_one:
                pool.sem_inc(s, 1)
            pool.sem_inc(y_stored, Y_START)
            pool.sem_inc(mx_ready, X_START)
            pool.sem_inc(started, 4)
            pool.memset(ident[:, :], 0.0).then_inc(pool_chain, 1)
            pool.memset(causal[:, :], 0.0).then_inc(pool_chain, 1)
            pool.memset(tri[:, :], 1.0).then_inc(pool_chain, 1)
            pool.memset(tok_idx[:, E * ECAP:], 0).then_inc(pool_chain, 1)
            pool.iota(pairs_i[:, :], pattern=[[ECAP * P, E]], base=1, channel_multiplier=0).then_inc(pool_chain, 1)
            pool.iota(tok_all[:, :], pattern=[[P, TILES]], base=0, channel_multiplier=1).then_inc(pool_chain, 1)
            pool.wait_ge(pool_chain, 6)
            pool.affine_select(out=ident[:, :], in_=ident[:, :], compare_op=ALU.not_equal, fill=1.0,
                               base=0, pattern=[[-1, P]], channel_multiplier=1).then_inc(consts_ready, 1)
            pool.affine_select(out=causal[:, :], in_=causal[:, :], compare_op=ALU.is_ge, fill=MASKED,
                               base=0, pattern=[[-1, P]], channel_multiplier=1).then_inc(consts_ready, 1)
            pool.affine_select(out=tri[:, :], in_=tri[:, :], compare_op=ALU.is_gt, fill=0.0,
                               base=0, pattern=[[1, P]], channel_multiplier=-1).then_inc(consts_ready, 1)
            pool.memset(zeros[:, :], 0).then_inc(consts_ready, 1)
            pool.wait_ge(consts_ready, 4)
            pool.tensor_copy(ident_r[:, :], ident[:, :]).then_inc(consts_ready, 1)
            pool.tensor_copy(causal_r[:, :], causal[:, :]).then_inc(consts_ready, 1)
            pool.tensor_copy(before[:, :], tri[:, :]).then_inc(consts_ready, 1)
            pool.memset(ones[:, :].bitcast(F32), 1.0).then_inc(consts_ready, 1)
            pool.memset(scan_ones[:, :], 1.0).then_inc(consts_ready, 1)
            pool.memset(seen[:, 0, :], 0.0).then_inc(consts_ready, 1)
            pool.tensor_copy(row_base[:, :], pairs_i[:, :]).then_inc(consts_ready, 1)
            for e in range(NSH):
                pool.wait_ge(ew_hi, e + 1)
                pool.tensor_tensor(lo_slot(e), eraw[:, e, :], hi_slot(e).bitcast(F32), ALU.subtract).then_inc(ew_lo, 1)
            pool.wait_ge(tok_zeroed, 16)
            with pool.Fori(0, B) as b:
                pool.tensor_copy(tok_s[:, :], tok_all[:, bass.ds(b * NT, NT)]).then_inc(tok_copied, 1)
                pool.wait_ge(tok_copied, past(b + 1))
                pool.wait_ge(tok_pos_ready, b + 1)
                settle(pool)
                for t in range(NT):
                    for k in range(TOPK):
                        pool.indirect_dma_start(
                            out=tok_d, out_offset=bass.IndirectOffsetOnAxis(ap=tok_pos[:, t, k:k + 1], axis=0),
                            in_=tok_s[:, t:t + 1], in_offset=None).then_inc(tok_out, 16)
                pool.wait_ge(tok_out, (b + 1) * (SCATTERS * 16))
            pool.wait_ge(pairs_ready, 1)
            pool.wait_ge(tok_in, 16)
            pool.wait_ge(y_added, past(B * YA))

            def gather_pairs(e, s, lo, hi, es):
                with pool.Fori(lo, hi) as p:
                    pool.wait_ge(mx_ready, p * ROWS + (X_START - ROWS))
                    col = nc.s_assert_within(e * ECAP + (p - lo) * ROWS, 0, E * ECAP,
                                             skip_runtime_bounds_check_because="an expert has at most T tokens")
                    for slot in range(2):
                        with pool.If(p % 2 == slot):
                            pool.tensor_copy(pair_idx[:, slot, :], tok_idx[:, bass.ds(col, ROWS)]).then_inc(idx_ready, 1)
                            pool.wait_ge(idx_ready, p + 1)
                            settle(pool)
                            for r in range(ROWS):
                                pool.indirect_dma_start(
                                    out=xg[:, slot, r, :], out_offset=None, in_=xn_d,
                                    in_offset=bass.IndirectOffsetOnAxis(ap=pair_idx[:, slot, r:r + 1], axis=0)
                                ).then_inc(xg_in[slot], 16)

            over_experts(pool, gather_pairs, row=1)
            with pool.Fori(0, B) as b:
                with pool.Fori(0, GROUPS) as g:
                    n = b * GROUPS + g
                    pool.wait_ge(y_stored, past((PAIRS + 1) * 16, Y_START))
                    pool.wait_ge(y_rows_ready, B)
                    pool.wait_ge(comb_added, past(n * NCOMB))
                    tiles = NT // GROUPS
                    src = y_rows[:, bass.ds(b * NT + g * tiles, tiles), 0:TOPK]
                    pool.tensor_copy(comb_idx[:, :].rearrange("p (t k) -> p t k", k=TOPK), src).then_inc(comb_idx_ready, 1)
                    pool.wait_ge(comb_idx_ready, n + 1)
                    settle(pool)
                    for j in range(NCOMB):
                        if j >= COMB:
                            pool.wait_ge(comb_added, past(n * NCOMB + j - COMB + 1))
                            settle(pool, j)
                        pool.indirect_dma_start(
                            out=comb[:, j % COMB, :], out_offset=None, in_=y_d,
                            in_offset=bass.IndirectOffsetOnAxis(ap=comb_idx[:, j:j + 1], axis=0)
                        ).then_inc(comb_in[j % COMB], 16)

        @block.tensor
        def _(pe):
            pe.wait_ge(started, 4)

            def split_product(out_, lhs, rhs, parts, n_inc, first=True, last=True):
                for k in range(parts):
                    (lh, ll), (rh, rl) = lhs(k), rhs(k)
                    pe.matmul(out_, lh, rh, start=(first and k == 0), stop=False)
                    pe.matmul(out_, lh, rl, start=False, stop=False)
                    mm = pe.matmul(out_, ll, rh, start=False, stop=(last and k == parts - 1))
                if n_inc is not None:
                    mm.then_inc(n_inc, 1)
                return mm

            pe.wait_ge(consts_ready, 11)
            pe.wait_ge(consts_in, 32)

            def hidden(turn, u):
                e, c = divmod(u, NC)
                pe.wait_ge(relu_ready, past((turn * UNITS + (u - 1 if u >= 2 else 0)) * KM))
                cs = slice(c * C, (c + 1) * C)
                for m in range(KM):
                    ms = slice(m * P, (m + 1) * P)
                    split_product(ps_s[:, 2 * (u % 2) + m, :],
                                  lambda k: (w1(hi_slot(e))[:, k, ms], w1(lo_slot(e))[:, k, ms]),
                                  lambda k: (xT_hi[:, k, cs], xT_lo[:, k, cs]), KD, h_ready)

            def outputs(turn, u):
                e, c = divmod(u, NC)
                pe.wait_ge(hhi_ready, (turn * UNITS + u + 1) * KM)
                pe.wait_ge(hlo_ready, past(turn * UNITS + u + 1))
                for q in range(CQ):
                    pe.wait_ge(y_added, past((turn * UNITS + u) * CQ - (CQ - 1 - q if u else 0)))
                    qs = slice(q * P, (q + 1) * P)
                    split_product(banks[q][:, :],
                                  lambda m: (h_hi[:, u % 2, m, qs], h_lo[:, u % 2, m, qs]),
                                  lambda m: (w2(hi_slot(e))[:, m, :], w2(lo_slot(e))[:, m, :]), KM, y_ready)

            def transpose_tile(bank, t):
                for k in range(KD):
                    mm = pe.transpose(bank[:, k * P:(k + 1) * P], xn[:, t, k * P:(k + 1) * P], ident[:, :])
                mm.then_inc(xnT_ready, 1)

            with pe.Fori(0, B) as b:
                for t in range(NT + 1):
                    if t < NT:
                        pe.wait_ge(xn_ready, b * NT + t + 1)
                        if t >= 2:
                            pe.wait_ge(xf_ready, past(b * NT + t - 1))
                        transpose_tile(ps_t[t % 2], t)
                    if t:
                        pe.wait_ge(xf_ready, past(b * NT + t))
                        for k in range(KD):
                            mm = pe.matmul(ps_logit[:, (t - 1) * E:t * E], xf[:, (t - 1) % 2, k, :], wr_sb[:, k, :],
                                           start=(k == 0), stop=(k == KD - 1))
                        mm.then_inc(logits_ready, 1)
                with pe.If(b == B - 1):
                    pe.wait_ge(xhi_ready, NT)
                    pe.wait_ge(xlo_ready, past(NT))
                    pe.wait_ge(ew_lo, NSH)
                    hidden(0, 0)
                pe.wait_ge(sel_ready, b + 1)
                pe.wait_ge(ranks_read, past(b))
                rsel_all = rsel[:, :, :].rearrange("p t e -> p (t e)")
                pe.matmul(ps_rank[:, 0:NT * E], before[:, :], rsel_all, start=True, stop=True)
                pe.matmul(ps_rank[:, NT * E:2 * NT * E], ones[:, :], rsel_all, start=True, stop=True).then_inc(ranks_ready, 1)

            with pe.Fori(0, B) as turn:
                with pe.If(turn == 1):
                    pe.wait_ge(xlo_ready, past(2 * NT))
                    hidden(turn, 0)
                hidden(turn, 1)
                pe.wait_ge(ranks_read, past(B))
                outputs(turn, 0)
                for u in range(2, UNITS):
                    hidden(turn, u)
                    outputs(turn, u - 1)
                with pe.If(turn == 0):
                    pe.wait_ge(x_in, (B + 1) * 16)
                    pe.wait_ge(relu_ready, past((UNITS - 1) * KM))
                    for t in range(NT):
                        if t >= 2:
                            pe.wait_ge(xlo_ready, past(NT + t - 1))
                        transpose_tile(ps_s[:, t % 2, :], t)
                outputs(turn, UNITS - 1)

            def transpose_pair(q):
                pe.wait_ge(mx_lo, q * ROWS)
                for slot in range(2):
                    with pe.If(q % 2 == slot):
                        pe.wait_ge(xg_in[slot], (q // 2 + 1) * (ROWS * 16))
                        for r in range(ROWS):
                            for k in range(KD):
                                mm = pe.transpose(ps_x[r][:, k * P:(k + 1) * P], xg[:, slot, r, k * P:(k + 1) * P],
                                                  ident[:, :])
                            mm.then_inc(mx_ready, 1)

            pe.wait_ge(pairs_ready, 1)
            pe.wait_ge(xg_in[0], ROWS * 16)
            for r in range(ROWS):
                for k in range(KD):
                    mm = pe.transpose(ps_x[r][:, k * P:(k + 1) * P], xg[:, 0, r, k * P:(k + 1) * P], ident[:, :])
                mm.then_inc(mx_ready, 1)

            def expert_pairs(e, s, lo, hi, es):
                w_hi, w_lo = hi_slot(s), lo_slot(s)
                with pe.Fori(lo, hi) as p:
                    pe.wait_ge(ew_lo, e + (NSH + 1))
                    pe.wait_ge(mx_lo, (p + 1) * ROWS)
                    pe.wait_ge(mrelu_ready, past(p * KM))
                    for m in range(KM):
                        ms = slice(m * P, (m + 1) * P)
                        split_product(ps_s[:, m, 0:PR],
                                      lambda k: (w1(w_hi)[:, k, ms], w1(w_lo)[:, k, ms]),
                                      lambda k: (xgT_hi[:, k, :], xgT_lo[:, k, :]), KD, mh_ready)
                    transpose_pair(p + 1)
                    pe.wait_ge(y0_copied, past(p + 1))
                    pe.wait_ge(y1_copied, past(p + 1))
                    for m in range(KM):
                        pe.wait_ge(mhlo_ready, past(p * KM + m + 1))
                        for r in range(ROWS):
                            rs_ = slice(r * P, (r + 1) * P)
                            split_product(ps_y[r][:, :], lambda _: (mh_hi[:, m, rs_], mh_lo[:, m, rs_]),
                                          lambda _: (w2(w_hi)[:, m, :], w2(w_lo)[:, m, :]), 1,
                                          my_ready if m == KM - 1 else None, first=(m == 0), last=(m == KM - 1))

            over_experts(pe, expert_pairs)
            def attend_pe(steps, this, g=None):
                for kind, i, a, after in steps:
                    n = this + after
                    unit = i * HPG + a
                    if kind in "KPQ":
                        j = {"K": a, "P": NC + a, "Q": 2 * NC + i * HPG + a}[kind]
                        if j == 0:
                            pe.wait_ge(aw_hi, past(n * PIECES + 3))
                            pe.wait_ge(aw_lo, past(n * PIECES + 3))
                            pe.wait_ge(exp_ready, past(n * N_UNITS))
                        if j in (2, 3):
                            pe.wait_ge(proj_lo, n * SPLIT + j - 1)
                        elif j in (4, 5):
                            pe.wait_ge(proj_hi, n * PROJ + j - 1)
                        elif j >= 6:
                            pe.wait_ge(proj_lo, n * SPLIT + j - 1 - NC)
                        cols = {"K": lambda w: wkv(w)[:, :, 0:HD], "P": lambda w: wkv(w)[:, :, HD:2 * HD],
                                "Q": lambda w: wq(w)[:, :, a * HD:(a + 1) * HD]}[kind]
                        c = i if kind == "Q" else a
                        cs = slice(c * C, (c + 1) * C)
                        split_product(ps_s[:, 1 + 2 * (j % 2), :], lambda k: (cols(wa_hi)[:, k, :], cols(wa_lo)[:, k, :]),
                                      lambda k: (xT_hi[:, k, cs], xT_lo[:, k, cs]), KD, proj_ready)
                    elif kind == "X":
                        for c in range(NC):
                            pe.wait_ge(proj_hi, n * PROJ + NC + c + 1)
                            for q in range(C // P):
                                mm = pe.transpose(ps_t[c][:, q * P:(q + 1) * P], vT[:, c, q * P:(q + 1) * P],
                                                  ident[:, :])
                            mm.then_inc(vtr_ready, 1)
                    elif kind == "S":
                        if a == 0 and i in (0, NT // 2):
                            pe.wait_ge(proj_lo, n * SPLIT + NC + (i // (NT // 2) + 1) * HPG)
                        if unit >= 2:
                            pe.wait_ge(exp_ready, past(n * N_UNITS + unit - 1))
                        keys = (i + 1) * P
                        half, at = divmod(i, NT // 2)
                        qs = slice(at * P, (at + 1) * P)
                        for c0 in range(0, keys, 512):
                            c1 = min(c0 + 512, keys)
                            o = ps_s[:, 2 * (unit % 2) + c0 // 512, 0:c1 - c0]
                            q_h, q_l, ks = qT_hi[:, half, a, qs], qT_lo[:, half, a, qs], slice(c0, c1)
                            pe.matmul(o, q_h, kT_hi[:, ks], start=True, stop=False)
                            if c1 == keys:
                                pe.matmul(o[:, c1 - c0 - P:c1 - c0], ident_r[:, :], causal_r[:, :],
                                          start=False, stop=False, skip_group_check=True)
                            pe.matmul(o, q_h, kT_lo[:, ks], start=False, stop=False)
                            mm = pe.matmul(o, q_l, kT_hi[:, ks], start=False, stop=True)
                        mm.then_inc(scores_ready, 1)
                    elif kind == "T":
                        blk = blocks_before(i) + a
                        pe.wait_ge(probs_ready, n * N_UNITS + (i + 1) * HPG)
                        if blk == 0:
                            pe.wait_ge(v_lo_ready, n * NC + NC)
                        if blk >= 2:
                            pe.wait_ge(pt_lo_ready, n * TRI + blk - 1)
                        for h in range(HPG):
                            mm = pe.transpose(ps_t[blk % 2][:, h * P:(h + 1) * P],
                                              probs[:, i % 2, h, a * P:(a + 1) * P], ident[:, :])
                        mm.then_inc(pt_ready, 1)
                    elif kind == "V":
                        blk = blocks_before(i) + a
                        pe.wait_ge(pt_lo_ready, n * TRI + blk + 1)
                        if a == 0:
                            pe.wait_ge(ctx_lo_ready, past(n * NT + i))
                        split_product(ps_ctx[:, :], lambda k: (v_hi[:, a, :], v_lo[:, a, :]),
                                      lambda k: (pT_hi[:, blk % RING, :], pT_lo[:, blk % RING, :]), 1, pv_done,
                                      first=(a == 0), last=(a == i))
                    elif kind == "D":
                        if i == 0:
                            pe.wait_ge(aw_lo, past((n + 1) * PIECES))
                        pe.wait_ge(ctx_lo_ready, past(n * NT + i + 1))
                        pe.wait_ge(dense_added, past(n * NT + i))
                        split_product(ps_d[:, :],
                                      lambda h: (cT_hi[:, h * P:(h + 1) * P], cT_lo[:, h * P:(h + 1) * P]),
                                      lambda h: (wd(wa_hi)[:, h, :], wd(wa_lo)[:, h, :]), HPG, dense_ready)

            pe.wait_ge(room_free, 2)
            with pe.Fori(0, B) as turn:
                with pe.If(turn == 1):
                    pe.wait_ge(xn_in, 32)
                    for t in range(NT):
                        if t >= 2:
                            pe.wait_ge(xr_lo, t - 1)
                        half, at = divmod(t, NT // 2)
                        for k in range(KD):
                            mm = pe.transpose(ps_t[t % 2][:, k * P:(k + 1) * P],
                                              xn_again[half][:, at, k * P:(k + 1) * P], ident[:, :])
                        mm.then_inc(xr_ready, 1)
                    pe.wait_ge(xr_lo, NT)
                attend_groups(pe, attend_pe, turn)

        @block.scalar
        def _(act):
            act.wait_ge(started, 4)
            for e in range(NSH):
                act.wait_ge(eraw_in[e], 16)
                act.activation(hi_slot(e), eraw[:, e, :], ACT.Copy).then_inc(ew_hi, 1)
            with act.Fori(0, B) as b:
                act.wait_ge(std_ready, b * 2 + 1)
                act.activation(std[:, :], rstd[:, :], ACT.Sqrt).then_inc(std_ready, 1)

                def copy_tile(t):
                    act.wait_ge(xnT_ready, b * NT + t + 1)
                    act.wait_ge(logits_ready, past(b * NT + max(t - 1, 0)))
                    act.activation(xf[:, t % 2, :, :], ps_t[t % 2][:, :].rearrange("p (k n) -> p k n", k=KD),
                                   ACT.Copy).then_inc(xf_ready, 1)

                with act.If(b < B - 1):
                    for t in range(NT):
                        copy_tile(t)
                with act.If(b == B - 1):
                    for t in range(NT):
                        if t >= 2:
                            act.wait_ge(xlo_ready, past(t - 1))
                        copy_tile(t)
                        act.wait_ge(xf_ready, past(b * NT + t + 1))
                        act.activation(xT_hi[:, :, t * P:(t + 1) * P], xf[:, t % 2, :, :], ACT.Copy).then_inc(xhi_ready, 1)
                act.wait_ge(z_ready, b + 1)
                act.activation(rs[:, :, :], rz[:, :, :], ACT.Exp, scale=-1.0).then_inc(ez_ready, 1)
            with act.Fori(0, B) as turn:
                for u in range(UNITS):
                    for m in range(KM):
                        act.wait_ge(h_ready, (turn * UNITS + u) * KM + m + 1)
                        act.wait_ge(hsq_ready, past(turn * UNITS + (u - 1 if u >= 2 else 0)))
                        act.activation(relu[:, u % 2, m, :], ps_s[:, 2 * (u % 2) + m, :], ACT.Relu).then_inc(relu_ready, 1)
                    act.wait_ge(y_ready, past((turn * UNITS + (u - 1 if u >= 2 else 0)) * CQ))
                    for m in range(KM):
                        act.wait_ge(relu_ready, past((turn * UNITS + u) * KM + m + 1))
                        act.activation(h_hi[:, u % 2, m, :], relu[:, u % 2, m, :], ACT.Square).then_inc(hhi_ready, 1)
                with act.If(turn == 0):
                    for t in range(NT):
                        act.wait_ge(xnT_ready, B * NT + t + 1)
                        act.activation(xT_hi[:, :, t * P:(t + 1) * P],
                                       ps_s[:, t % 2, :].rearrange("p (k n) -> p k n", k=KD), ACT.Copy).then_inc(xhi_ready, 1)

            act.wait_ge(pairs_ready, 1)
            act.wait_ge(xn_out, 16 * B)
            act.wait_ge(y_ready, past(B * YA))
            act.wait_ge(y_rows_ready, B)

            def upper_tokens(q):
                for r in range(ROWS):
                    act.wait_ge(mx_ready, q * ROWS + (r + 1 + X_START))
                    act.activation(xgT_hi[:, :, r * P:(r + 1) * P], ps_x[r].rearrange("p (k n) -> p k n", k=KD),
                                   ACT.Copy).then_inc(mx_hi, 1)

            def upper_weights(e, slot, es=None):
                n_in = (slot // 2 + NSH // 2 + 1) * 16 if es is None else None
                act.wait_ge(eraw_in[slot % 2], n_in if es is None else (e // 2 + (NSH // 2 + 1)) * 16)
                act.activation(hi_slot(slot), eraw[:, slot % 2, :], ACT.Copy).then_inc(ew_hi, 1)

            def copy_output(q):
                act.wait_ge(my_ready, past(q * ROWS))
                act.wait_ge(y_stored, past((q - 2) * 16, Y_START))
                act.activation(ysb[:, bass.ds((q + 1) % 2, 1), 1, :].rearrange("p s d -> p (s d)"), ps_y[1][:, :],
                               ACT.Copy).then_inc(y1_copied, 1)

            upper_weights(0, 0)
            upper_weights(1, 1)
            upper_tokens(0)

            def expert_uppers(e, s, lo, hi, es):
                upper_weights(e + 2, (s + 2) % SLOTS, es)
                with act.Fori(lo, hi) as p:
                    copy_output(p)
                    for m in range(KM):
                        act.wait_ge(mh_ready, p * KM + m + 1)
                        act.wait_ge(mhsq_ready, past(p * KM))
                        act.activation(mrelu[:, m, :], ps_s[:, m, 0:PR], ACT.Relu).then_inc(mrelu_ready, 1)
                        act.wait_ge(mrelu_ready, past(p * KM + m + 1))
                        act.activation(mh_hi[:, m, :], mrelu[:, m, :], ACT.Square).then_inc(mhhi_ready, 1)
                    upper_tokens(p + 1)

            over_experts(act, expert_uppers)
            copy_output(pair_bound(act, E))
            def attend_act(steps, this, g=None):
                for kind, i, a, after in steps:
                    n = this + after
                    if kind == "W":
                        in_slot = PIECES - PIECES // 2 if a % 2 == 0 else PIECES // 2
                        act.wait_ge(araw_in[a % 2], n * (16 * in_slot) + 16 * (a // 2 + 1))
                        if a == 3:
                            act.wait_ge(dense_ready, past(n * NT))
                        act.activation(wa_hi[:, a * PIECE:(a + 1) * PIECE], araw[:, a % 2, :],
                                       ACT.Copy).then_inc(aw_hi, 1)
                    elif kind == "K":
                        act.wait_ge(proj_ready, n * PROJ + a + 1)
                        act.activation(kT_hi[:, a * C:(a + 1) * C], ps_s[:, 1 + 2 * (a % 2), :],
                                       ACT.Copy).then_inc(proj_hi, 1)
                    elif kind == "P":
                        act.wait_ge(proj_ready, n * PROJ + NC + a + 1)
                        act.activation(vT[:, a, :], ps_s[:, 1 + 2 * (a % 2), :], ACT.Copy).then_inc(proj_hi, 1)
                    elif kind == "Q":
                        j = 2 * NC + i * HPG + a
                        act.wait_ge(proj_ready, n * PROJ + j + 1)
                        act.activation(qT_hi[:, i, a, :], ps_s[:, 1 + 2 * (j % 2), :], ACT.Copy,
                                       scale=SCALE).then_inc(proj_hi, 1)
                    elif kind == "X":
                        for c in range(NC):
                            act.wait_ge(vtr_ready, n * NC + c + 1)
                            act.activation(v_hi[:, c * (C // P):(c + 1) * (C // P), :],
                                           ps_t[c][:, :].rearrange("p (q d) -> p q d", q=C // P),
                                           ACT.Copy).then_inc(v_hi_ready, 1)
                    elif kind == "E":
                        unit = i * HPG + a
                        act.wait_ge(max_ready, n * N_UNITS + unit + 1)
                        if i >= 2:
                            act.wait_ge(pt_ready, n * TRI + blocks_before(i - 1))
                        keys = (i + 1) * P
                        s = 2 * (unit % 2)
                        src = ps_s[:, s:s + 2, :].rearrange("p c n -> p (c n)")[:, 0:keys]
                        act.activation(probs[:, i % 2, a, 0:keys], src, ACT.Exp, bias=negmax[:, i % 2, a:a + 1],
                                       accum_out=rowsum[:, i % 2, a:a + 1]).then_inc(exp_ready, 1)
                    elif kind == "T":
                        blk = blocks_before(i) + a
                        act.wait_ge(pt_ready, n * TRI + blk + 1)
                        if blk >= RING:
                            act.wait_ge(pv_done, n * TRI + blk - RING + 1)
                        act.activation(pT_hi[:, blk % RING, :], ps_t[blk % 2][:, :], ACT.Copy).then_inc(pt_hi_ready, 1)
                    elif kind == "F":
                        act.wait_ge(pv_done, n * TRI + blocks_before(i + 1))
                        act.wait_ge(dense_ready, past(n * NT + i))
                        act.activation(cT_hi[:, :], ps_ctx[:, :], ACT.Copy).then_inc(ctx_hi_ready, 1)

            act.wait_ge(room_free, 2)
            with act.Fori(0, B) as turn:
                with act.If(turn == 1):
                    for t in range(NT):
                        act.wait_ge(xr_ready, t + 1)
                        if t == 0:
                            act.wait_ge(y_stored, past((PAIRS + 1) * 16, Y_START))
                        act.activation(xT_hi[:, :, t * P:(t + 1) * P],
                                       ps_t[t % 2][:, :].rearrange("p (k n) -> p k n", k=KD), ACT.Copy).then_inc(xr_hi, 1)
                attend_groups(act, attend_act, turn)

        @block.vector
        def _(dve):
            LINKS = 45
            dve.wait_ge(started, 4)

            def subtract(out_, whole, upper, signal):
                dve.tensor_tensor(out_, whole, upper.bitcast(F32), ALU.subtract).then_inc(signal, 1)

            dve.wait_ge(consts_ready, 11)
            with dve.Fori(0, B) as b:
                base = b * LINKS
                link = [0]

                def chain(ins):
                    link[0] += 1
                    ins.then_inc(ln_chain, 1)
                    dve.wait_ge(ln_chain, base + link[0])

                def hold():
                    dve.memset(rcross[:, 0:1], 0.0)

                dve.wait_ge(x_in, b * 16 + 16)
                for t in range(NT):
                    last = dve.bn_stats(stats[:, t, :], xn[:, t, :])
                chain(last)
                hold()
                for t in range(NT):
                    last = dve.bn_aggr(mv[:, t, :], stats[:, t, :])
                chain(last)
                dve.tensor_scalar(rstd[:, :], mv[:, :, 1], EPS, None, ALU.add).then_inc(std_ready, 1)
                dve.wait_ge(std_ready, b * 2 + 2)
                chain(dve.reciprocal(rstd[:, :], std[:, :]))
                for t in range(NT):
                    dve.tensor_scalar(xn[:, t, :], xn[:, t, :], mv[:, t, 0:1], rstd[:, t:t + 1],
                                      ALU.subtract, ALU.mult).then_inc(xn_ready, 1)
                with dve.If(b == B - 1):
                    for t in range(NT):
                        dve.wait_ge(xhi_ready, t + 1)
                        subtract(xT_lo[:, :, t * P:(t + 1) * P], xf[:, t % 2, :, :], xT_hi[:, :, t * P:(t + 1) * P], xlo_ready)
                dve.wait_ge(logits_ready, past(b * NT + NT))
                dve.wait_ge(consts_in, 32)
                dve.tensor_tensor(rz[:, :, :], ps_logit[:, 0:NT * E].rearrange("p (t e) -> p t e", t=NT),
                                  br_sb[:, :].unsqueeze(1).to_broadcast([P, NT, E]), ALU.add).then_inc(z_ready, 1)
                dve.wait_ge(ez_ready, b + 1)
                chain(dve.tensor_scalar(rs[:, :, :], rs[:, :, :], 1.0, None, ALU.add))
                chain(dve.reciprocal(rs[:, :, :], rs[:, :, :]))
                pairs = rs[:, :, :].rearrange("p t (g a c) -> p (t g) a c", g=G, a=2)
                chain(dve.tensor_tensor(rhi[:, :, :], pairs[:, :, :, 0], pairs[:, :, :, 1], ALU.max))
                chain(dve.tensor_tensor(rlo[:, :, :], pairs[:, :, :, 0], pairs[:, :, :, 1], ALU.min))
                chain(dve.tensor_tensor(rlo[:, :, :], rlo[:, :, :], rhi[:, :, :], ALU.add))
                chain(dve.tensor_tensor(rcross[:, :], rhi[:, :, 0], rhi[:, :, 1], ALU.add))
                chain(dve.tensor_tensor(rgw[:, :], rlo[:, :, 0], rlo[:, :, 1], ALU.max))
                chain(dve.tensor_tensor(rgw[:, :], rgw[:, :], rcross[:, :], ALU.max))
                hold()
                for t in range(NT):
                    last = dve.max(out=top_g[:, t, :], in_=rgw[:, t * G:(t + 1) * G])
                chain(last)
                chain(dve.memset(top_g[:, :, KG:8], -1.0))
                hold()
                for t in range(NT):
                    last = dve.match_replace(out=rgm[:, t * G:(t + 1) * G], in_to_replace=top_g[:, t, :],
                                             in_values=rgw[:, t * G:(t + 1) * G], imm_value=-2.0)
                chain(last)
                chain(dve.tensor_scalar(rgm[:, :], rgm[:, :], -2.0, None, ALU.is_equal))
                chain(dve.tensor_tensor(rmask[:, :, :].rearrange("p t (g c) -> p (t g) c", g=G),
                                        rs[:, :, :].rearrange("p t (g c) -> p (t g) c", g=G),
                                        rgm[:, :].unsqueeze(2).to_broadcast([P, NT * G, EG]), ALU.mult))
                hold()
                for t in range(NT):
                    last = dve.max(out=top_e[:, t, :], in_=rmask[:, t, :])
                chain(last)
                chain(dve.memset(top_e[:, :, TOPK:8], -1.0))
                hold()
                for t in range(NT):
                    last = dve.match_replace(out=rz[:, t, :], in_to_replace=top_e[:, t, :],
                                             in_values=rmask[:, t, :], imm_value=-2.0)
                chain(last)
                chain(dve.tensor_scalar(rsel[:, :, :], rz[:, :, :], -2.0, None, ALU.is_equal))
                dve.memset(rcross[:, 0:1], 0.0).then_inc(sel_ready, 1)
                sel = rsel[:, :, :].bitcast(F32)
                chain(dve.tensor_tensor(rz[:, :, :], sel, rs[:, :, :], ALU.mult))
                chain(dve.tensor_reduce(rsum[:, :], rz[:, :, :], AX.X, ALU.add))
                chain(dve.tensor_scalar(rsum[:, :], rsum[:, :], 1e-20, None, ALU.add))
                chain(dve.reciprocal(rsum[:, :], rsum[:, :]))
                chain(dve.scalar_tensor_tensor(out=gate[:, :, :], in0=rz[:, :, :], scalar=ROUTE_SCALE,
                                               in1=rsum[:, :].unsqueeze(2).to_broadcast([P, NT, E]),
                                               op0=ALU.mult, op1=ALU.mult))
                dve.wait_ge(ranks_ready, b + 1)
                ranks = ps_rank[:, 0:NT * E].rearrange("p (t e) -> p t e", t=NT)
                for t in range(NT):
                    chain(dve.tensor_tensor(seen[:, t + 1, :], seen[:, t, :],
                                            ps_rank[:, (NT + t) * E:(NT + t + 1) * E], ALU.add))
                chain(dve.tensor_tensor(rrow[:, :, :], seen[:, 0:NT, :], ranks, ALU.add))
                dve.tensor_copy(seen[:, 0, :], seen[:, NT, :]).then_inc(ranks_read, 1)
                chain(dve.tensor_tensor(rrow[:, :, :], rrow[:, :, :],
                                        row_base[:, :].unsqueeze(1).to_broadcast([P, NT, E]), ALU.add))
                chain(dve.tensor_tensor(rrow[:, :, :], rrow[:, :, :], sel, ALU.mult))
                hold()
                for t in range(NT):
                    last = dve.max(out=top_y[:, t, :], in_=rrow[:, t, :])
                chain(last)
                chain(dve.tensor_scalar(yrow_s[:, :, :], top_y[:, :, :], -1.0, None, ALU.add))
                chain(dve.tensor_scalar(bits[:, 0, :, :], yrow_s[:, :, :], P - 1, 4,
                                        ALU.bitwise_and, ALU.logical_shift_left))
                chain(dve.tensor_scalar(bits[:, 1, :, :], yrow_s[:, :, :], 7, ECAP - 1,
                                        ALU.logical_shift_right, ALU.bitwise_and))
                chain(dve.tensor_tensor(bits[:, 0, :, :], bits[:, 0, :, :], bits[:, 1, :, :], ALU.bitwise_or))
                chain(dve.tensor_scalar(bits[:, 1, :, :], yrow_s[:, :, :], E * T - T, None, ALU.bitwise_and))
                dve.wait_ge(tok_copied, past(b + 1))
                dve.tensor_tensor(tok_pos[:, :, :], bits[:, 0, :, :], bits[:, 1, :, :],
                                  ALU.bitwise_or).then_inc(tok_pos_ready, 1)
                dve.tensor_copy(y_rows[:, bass.ds(b * NT, NT), :], yrow_s[:, :, :])
                chain(dve.tensor_tensor(match[:, :, :, :],
                                        rrow[:, :, :].unsqueeze(2).to_broadcast([P, NT, TOPK, E]),
                                        top_y[:, :, 0:TOPK].unsqueeze(3).to_broadcast([P, NT, TOPK, E]), ALU.is_equal))
                chain(dve.tensor_tensor(match[:, :, :, :], match[:, :, :, :],
                                        gate[:, :, :].unsqueeze(2).to_broadcast([P, NT, TOPK, E]), ALU.mult))
                chain(dve.tensor_reduce(y_gate[:, bass.ds(b * NT, NT), :], match[:, :, :, :], AX.X, ALU.add))
                assert link[0] == LINKS, link[0]

            ROW_LINKS = 6
            last_link = [0]

            def chain_end(ins):
                last_link[0] += 1
                ins.then_inc(ln_chain, 1)
                dve.wait_ge(ln_chain, LINKS * B + last_link[0])

            chain_end(dve.tensor_scalar(pairs_f[:, :], seen[:, 0, :], float(PR - 1), None, ALU.add))
            chain_end(dve.tensor_copy(pairs_i[:, :], pairs_f[:, :]))
            chain_end(dve.tensor_scalar(pairs_i[:, :], pairs_i[:, :], 8, None, ALU.logical_shift_right))
            chain_end(dve.tensor_copy(pairs_f[:, :], pairs_i[:, :]))
            chain_end(dve.tensor_scalar(pairs_f[:, :], pairs_f[:, :], 1.0, None, ALU.max))
            chain_end(dve.tensor_tensor_scan(scan_f[:, :], scan_ones[:, :], pairs_f[:, :], 0.0, ALU.mult, ALU.add))
            chain_end(dve.memset(first_pair[:, :, 0:1], 0))
            for row in range(2):
                chain_end(dve.tensor_copy(first_pair[:, row, 1:E + 1], scan_f[:, :]))
            dve.tensor_scalar(first_pair[:, 1, E:E + 1], scan_f[:, E - 1:E], 1.0, None, ALU.add).then_inc(pairs_ready, 1)
            dve.wait_ge(pairs_ready, 1)
            chain_end(dve.tensor_tensor(scan_f[:, :], scan_f[:, :], pairs_f[:, :], ALU.subtract))
            chain_end(dve.tensor_scalar(scan_f[:, :], scan_f[:, :], float(PR), None, ALU.mult))
            chain_end(dve.tensor_scalar(row_base[:, :], row_base[:, :], -1.0, None, ALU.add))
            chain_end(dve.tensor_tensor(scan_f[:, :], scan_f[:, :], row_base[:, :], ALU.subtract))

            def find_rows(b, step):
                rows = y_rows[:, bass.ds(b * NT, NT), :]
                at = LINKS * B + last_link[0] + b * ROW_LINKS
                link = [0 if step == 0 else 4]

                def chain(ins):
                    link[0] += 1
                    ins.then_inc(ln_chain, 1)
                    dve.wait_ge(ln_chain, at + link[0])

                if step == 0:
                    chain(dve.tensor_copy(top_y[:, :, :], rows))
                    chain(dve.tensor_scalar(yrow_s[:, :, :], rows, E * T - T, None, ALU.bitwise_and))
                    chain(dve.tensor_copy(top_e[:, :, :], yrow_s[:, :, :]))
                    chain(dve.tensor_tensor(match[:, :, :, :],
                                            top_e[:, :, 0:TOPK].unsqueeze(3).to_broadcast([P, NT, TOPK, E]),
                                            row_base[:, :].unsqueeze(1).unsqueeze(1).to_broadcast([P, NT, TOPK, E]),
                                            ALU.is_equal))
                else:
                    chain(dve.tensor_tensor(match[:, :, :, :], match[:, :, :, :],
                                            scan_f[:, :].unsqueeze(1).unsqueeze(1).to_broadcast([P, NT, TOPK, E]),
                                            ALU.mult))
                    chain(dve.tensor_reduce(top_e[:, :, 0:TOPK], match[:, :, :, :], AX.X, ALU.add))
                    dve.tensor_tensor(rows[:, :, 0:TOPK], top_y[:, :, 0:TOPK], top_e[:, :, 0:TOPK],
                                      ALU.add).then_inc(y_rows_ready, 1)

            def add_outputs(turn, u):
                e, c = divmod(u, NC)
                for q in range(CQ):
                    t = c * CQ + q
                    k = (turn * UNITS + u) * CQ
                    dve.wait_ge(y_ready, past(k + q + 1))
                    if u == 0 and q == 0:
                        dve.wait_ge(acc_in, (turn + 1) * 16)
                    dve.wait_ge(y_added, past(k + q + 1 - NT if u >= 2 else turn * YA))
                    dve.tensor_tensor(acc[:, t, :], banks[q][:, :], acc[:, t, :], ALU.add).then_inc(y_added, 1)

            with dve.Fori(0, B) as turn:
                for u in range(UNITS):
                    dve.wait_ge(relu_ready, past((turn * UNITS + u + 1) * KM))
                    dve.wait_ge(hlo_ready, past(turn * UNITS + u))
                    dve.tensor_tensor(hsq[:, :, :], relu[:, u % 2, :, :], relu[:, u % 2, :, :],
                                      ALU.mult).then_inc(hsq_ready, 1)
                    dve.wait_ge(hsq_ready, past(turn * UNITS + u + 1))
                    dve.wait_ge(hhi_ready, (turn * UNITS + u + 1) * KM)
                    subtract(h_lo[:, u % 2, :, :], hsq[:, :, :], h_hi[:, u % 2, :, :], hlo_ready)
                    if u >= 1:
                        add_outputs(turn, u - 1)
                    if u < 2:
                        find_rows(turn, u)
                with dve.If(turn == 0):
                    for t in range(NT):
                        dve.wait_ge(xhi_ready, NT + t + 1)
                        ts = slice(t * P, (t + 1) * P)
                        subtract(xT_lo[:, :, ts], ps_s[:, t % 2, :].rearrange("p (k n) -> p k n", k=KD),
                                 xT_hi[:, :, ts], xlo_ready)
                add_outputs(turn, UNITS - 1)

            dve.wait_ge(y_added, past(B * YA))
            dve.wait_ge(xn_out, 16 * B)

            def lower_tokens(q):
                for r in range(ROWS):
                    dve.wait_ge(mx_hi, q * ROWS + (r + 1))
                    rr = slice(r * P, (r + 1) * P)
                    subtract(xgT_lo[:, :, rr], ps_x[r].rearrange("p (k n) -> p k n", k=KD), xgT_hi[:, :, rr], mx_lo)

            def copy_output(q):
                dve.wait_ge(my_ready, past(q * ROWS))
                dve.wait_ge(y_stored, past((q - 2) * 16, Y_START))
                dve.tensor_copy(ysb[:, bass.ds((q + 1) % 2, 1), 0, :].rearrange("p s d -> p (s d)"),
                                ps_y[0][:, :]).then_inc(y0_copied, 1)

            for e in range(2):
                dve.wait_ge(ew_hi, NSH + e + 1)
                subtract(lo_slot(e), eraw[:, e, :], hi_slot(e), ew_lo)
            lower_tokens(0)

            def expert_lowers(e, s, lo, hi, es):
                dve.wait_ge(ew_hi, e + (NSH + 3))
                subtract(lo_slot((s + 2) % SLOTS), eraw[:, s % 2, :], hi_slot((s + 2) % SLOTS), ew_lo)
                with dve.Fori(lo, hi) as p:
                    copy_output(p)
                    for m in range(KM):
                        dve.wait_ge(mrelu_ready, past(p * KM + m + 1))
                        dve.wait_ge(mhlo_ready, past(p * KM))
                        dve.tensor_tensor(mhsq[:, m, :], mrelu[:, m, :], mrelu[:, m, :], ALU.mult).then_inc(mhsq_ready, 1)
                        dve.wait_ge(mhsq_ready, past(p * KM + m + 1))
                        dve.wait_ge(mhhi_ready, p * KM + m + 1)
                        subtract(mh_lo[:, m, :], mhsq[:, m, :], mh_hi[:, m, :], mhlo_ready)
                    lower_tokens(p + 1)

            over_experts(dve, expert_lowers)
            copy_output(pair_bound(dve, E))
            def attend_dve(steps, this, g, turn):
                combined = added = 0
                for kind, i, a, after in steps:
                    n = this + after
                    if kind == "W":
                        dve.wait_ge(aw_hi, past(n * PIECES + a + 1))
                        ws = slice(a * PIECE, (a + 1) * PIECE)
                        subtract(wa_lo[:, ws], araw[:, a % 2, :], wa_hi[:, ws], aw_lo)
                    elif kind == "K":
                        dve.wait_ge(proj_hi, n * PROJ + a + 1)
                        cs = slice(a * C, (a + 1) * C)
                        subtract(kT_lo[:, cs], ps_s[:, 1 + 2 * (a % 2), :], kT_hi[:, cs], proj_lo)
                    elif kind == "Q":
                        j = 2 * NC + i * HPG + a
                        dve.wait_ge(proj_hi, n * PROJ + j + 1)
                        dve.scalar_tensor_tensor(out=qT_lo[:, i, a, :], in0=ps_s[:, 1 + 2 * (j % 2), :],
                                                 scalar=SCALE, in1=qT_hi[:, i, a, :].bitcast(F32),
                                                 op0=ALU.mult, op1=ALU.subtract).then_inc(proj_lo, 1)
                    elif kind == "X":
                        for c in range(NC):
                            dve.wait_ge(v_hi_ready, n * NC + c + 1)
                            vs = slice(c * (C // P), (c + 1) * (C // P))
                            subtract(v_lo[:, vs, :], ps_t[c][:, :].rearrange("p (q d) -> p q d", q=C // P),
                                     v_hi[:, vs, :], v_lo_ready)
                    elif kind == "S":
                        unit = i * HPG + a
                        dve.wait_ge(scores_ready, n * N_UNITS + unit + 1)
                        s = 2 * (unit % 2)
                        src = ps_s[:, s:s + 2, :].rearrange("p c n -> p (c n)")[:, 0:(i + 1) * P]
                        dve.tensor_reduce(negmax[:, i % 2, a:a + 1], src, AX.X, ALU.max, negate=True).then_inc(max_ready, 1)
                    elif kind == "N":
                        dve.wait_ge(exp_ready, past(n * N_UNITS + i * HPG + a + 1))
                        dve.reciprocal(rnorm[:, i % 2, a:a + 1], rowsum[:, i % 2, a:a + 1]).then_inc(rnorm_ready, 1)
                        dve.wait_ge(rnorm_ready, n * N_UNITS + i * HPG + a + 1)
                        pr = probs[:, i % 2, a, 0:(i + 1) * P]
                        dve.tensor_scalar(pr, pr, rnorm[:, i % 2, a:a + 1], None, ALU.mult).then_inc(probs_ready, 1)
                    elif kind == "T":
                        blk = blocks_before(i) + a
                        dve.wait_ge(pt_hi_ready, n * TRI + blk + 1)
                        subtract(pT_lo[:, blk % RING, :], ps_t[blk % 2][:, :], pT_hi[:, blk % RING, :], pt_lo_ready)
                    elif kind == "F":
                        dve.wait_ge(ctx_hi_ready, n * NT + i + 1)
                        subtract(cT_lo[:, :], ps_ctx[:, :], cT_hi[:, :], ctx_lo_ready)
                    elif kind == "C":
                        j = i
                        at = g * (NT // GROUPS) + j // TOPK
                        if not (combined or added):
                            dve.wait_ge(z_in, past(turn * 16))
                        dve.wait_ge(dense_added, past(n * NT + added))
                        dve.wait_ge(comb_in[j % COMB], (n * (NCOMB // COMB) + j // COMB + 1) * 16)
                        dve.wait_ge(comb_added, past(n * NCOMB + j))
                        acc_t = acc[:, bass.ds(at, 1), :].rearrange("p t d -> p (t d)")
                        w_t = y_gate[:, bass.ds(turn * NT + at, 1), j % TOPK]
                        dve.scalar_tensor_tensor(out=acc_t, in0=comb[:, j % COMB, :], scalar=w_t, in1=acc_t,
                                                 op0=ALU.mult, op1=ALU.add).then_inc(comb_added, 1)
                        combined = j + 1
                    elif kind == "D":
                        dve.wait_ge(dense_ready, past(n * NT + i + 1))
                        if i == 0:
                            dve.wait_ge(dense_added, past(n * NT))
                        if not (combined or added):
                            dve.wait_ge(z_in, past(turn * 16))
                        dve.wait_ge(comb_added, past(n * NCOMB + combined))
                        dve.tensor_tensor(acc[:, i, :], acc[:, i, :], ps_d[:, :], ALU.add).then_inc(dense_added, 1)
                        added = i + 1

            dve.wait_ge(room_free, 2)
            with dve.Fori(0, B) as turn:
                with dve.If(turn == 1):
                    for t in range(NT):
                        dve.wait_ge(xr_hi, t + 1)
                        ts = slice(t * P, (t + 1) * P)
                        subtract(xT_lo[:, :, ts], ps_t[t % 2][:, :].rearrange("p (k n) -> p k n", k=KD), xT_hi[:, :, ts], xr_lo)
                attend_groups(dve, lambda steps, this, g=None: attend_dve(steps, this, g, turn), turn)


def kernel(L0_attn_x, L0_attn_w_q, L0_attn_w_kv, L0_attn_w_dense, L0_ffn_Wr, L0_ffn_br, L0_ffn_W1, L0_ffn_W2,
           L0_ffn_Ws1, L0_ffn_Ws2):
    import concourse.bacc as bacc
    from concourse.bass_utils import run_bass_kernel_spmd

    wq = np.asarray(L0_attn_w_q).reshape(KD, P, GROUPS, HPG * HD).transpose(2, 1, 0, 3).reshape(GROUPS, P, WQ_COLS)
    wkv = np.asarray(L0_attn_w_kv).reshape(KD, P, 2, GROUPS, HD).transpose(3, 1, 0, 2, 4).reshape(GROUPS, P, WKV_COLS)
    wd = np.asarray(L0_attn_w_dense).reshape(GROUPS, HPG, P, D).transpose(0, 2, 1, 3).reshape(GROUPS, P, WD_COLS)
    wa = np.ascontiguousarray(np.concatenate([wq, wkv, wd], axis=2).reshape(GROUPS * P, WA_COLS))
    w1 = np.concatenate([np.asarray(L0_ffn_W1), np.asarray(L0_ffn_Ws1).reshape(NSH, M, D)], axis=0)
    w1 = w1.reshape(E + NSH, M, KD, P).transpose(0, 3, 2, 1).reshape(E + NSH, P, KD * M)
    w2 = np.concatenate([np.asarray(L0_ffn_W2), np.asarray(L0_ffn_Ws2).reshape(D, NSH, M).transpose(1, 0, 2)], axis=0)
    w2 = w2.reshape(E + NSH, D, KM, P).transpose(0, 3, 2, 1).reshape(E + NSH, P, KM * D)
    we = np.concatenate([w1, w2], axis=2)
    we = np.ascontiguousarray(np.concatenate([we, we[:AHEAD - NSH]], axis=0).reshape((E + AHEAD) * P, W_COLS))
    wr = np.ascontiguousarray(np.asarray(L0_ffn_Wr).reshape(E, KD, P).transpose(2, 1, 0))
    br = np.ascontiguousarray(np.broadcast_to(np.asarray(L0_ffn_br), (P, E)))
    x = np.ascontiguousarray(L0_attn_x)

    nc = bacc.Bacc("TRN2", target_bir_lowering=False, num_devices=1)
    arrays = {"x": x, "wa": wa, "we": we, "wr": wr, "br": br}
    aps = [nc.dram_tensor(k, a.shape, mybir.dt.from_np(a.dtype), kind="ExternalInput").ap() for k, a in arrays.items()]
    out = nc.dram_tensor("out", (B, SQ, D), F32, kind="ExternalOutput").ap()
    moe_attention_kernel(nc, *aps, out)
    r = run_bass_kernel_spmd(nc, [arrays], core_ids=[0])
    return r.results[0]["out"]
```
